# Optimizing a Trainium2 kernel written in Bass

```python
import numpy as np
import jax
import jax.numpy as jnp

def _softmax(x, axis=-1):
    return jax.nn.softmax(x, axis=axis)

def _gelu(x):
    return jax.nn.gelu(x, approximate=True)

def _silu(x):
    return jax.nn.silu(x)

def _sigmoid(x):
    return jax.nn.sigmoid(x)

def _layernorm(x, axis=-1, eps=1e-05):
    m = jnp.mean(x, axis=axis, keepdims=True)
    v = jnp.var(x, axis=axis, keepdims=True)
    return (x - m) / jnp.sqrt(v + eps)

def _scatter_add(tgt, idx, src, axis=0):
    return tgt.at[idx].add(src)

def _segment_sum(src, seg, n):
    return jax.ops.segment_sum(src, seg, n)
kernel_name = 'mk_xattn_ffn_d1_seqx_r4_490dae'

def setup_inputs(seed: int=0):
    np.random.seed(seed)
    _w = jnp.asarray

    def _rec_inputs():
        import jax
        import jax.numpy as jnp
        _rk = jax.random.key(seed)
        x = 7.22e-05 + 1 * jax.random.normal(jax.random.fold_in(_rk, 1), (2, 1024, 256), jnp.float32)
        _lenS = 1024 - jax.random.randint(jax.random.fold_in(_rk, 7), (2,), 0, max(1, 1024 // 4) + 1, jnp.int32)
        _lenS2 = 77 - jax.random.randint(jax.random.fold_in(_rk, 8), (2,), 0, max(1, 77 // 4) + 1, jnp.int32)
        _ctx_1024P = jax.random.normal(jax.random.fold_in(_rk, 11), (2, 16, 256), jnp.float32)
        _ctx_1024c = jax.random.dirichlet(jax.random.fold_in(_rk, 511), 0.3 * jnp.ones((16,), jnp.float32), (2, 77))
        _ctx_1024t = jnp.einsum('bsk,bkd->bsd', _ctx_1024c, _ctx_1024P)
        _ctx_1024t = _ctx_1024t * jax.lax.rsqrt(jnp.mean(jnp.square(_ctx_1024t)) + 1e-12) * 0.953939
        ctx_1024 = 0.000227908 + 0.99994 * (_ctx_1024t + 0.3 * jax.random.normal(jax.random.fold_in(_rk, 611), (2, 77, 256), jnp.float32))
        return (x, ctx_1024)
    x, ctx_1024 = _rec_inputs()

    def _L0_xattn_setup():
        import jax, jax.numpy as jnp
        import numpy as np
        EMBED_DIM = 256
        N_HEAD = 16
        HEAD_DIM = EMBED_DIM // N_HEAD
        key = jax.random.key(seed)
        k1, k2, k3, k4, k5, k6 = jax.random.split(key, 6)
        B, T, MEM = (4, 512, 64)
        x = jax.random.normal(k1, (B, T, EMBED_DIM), dtype=jnp.float32)
        ext_mem = jax.random.normal(k2, (B, MEM, EMBED_DIM), dtype=jnp.float32)
        W_attn = jax.random.normal(k3, (EMBED_DIM, 3 * EMBED_DIM), dtype=jnp.float32) / np.sqrt(EMBED_DIM)
        b_attn = jax.random.normal(k4, (3 * EMBED_DIM,), dtype=jnp.float32) * 0.02
        W_proj = jax.random.normal(k5, (EMBED_DIM, EMBED_DIM), dtype=jnp.float32) / np.sqrt(EMBED_DIM)
        b_proj = jax.random.normal(k6, (EMBED_DIM,), dtype=jnp.float32) * 0.02
        return {'x': x, 'ext_mem': ext_mem, 'W_attn': W_attn, 'b_attn': b_attn, 'W_proj': W_proj, 'b_proj': b_proj}
    _L0_xattn_all = _L0_xattn_setup()
    _L0_xattn_in = {k: v for k, v in _L0_xattn_all.items() if k in ('W_attn', 'b_attn', 'W_proj', 'b_proj')}
    del _L0_xattn_all

    def _L0_ffn_setup():
        import jax, jax.numpy as jnp
        import numpy as np
        EPS = 1e-06
        LN_EPS = 1e-05

        def _absmean_core(W):
            gamma = jnp.mean(jnp.abs(W)) + EPS
            Ws = W / gamma
            Wq = jnp.sign(Ws) * jnp.minimum(jnp.round(jnp.abs(Ws)), 1.0)
            return (Wq, gamma)

        @jax.custom_vjp
        def absmean(W):
            return _absmean_core(W)[0]

        def _absmean_fwd(W):
            Wq, gamma = _absmean_core(W)
            return (Wq, gamma)

        def _absmean_bwd(gamma, g):
            return (g / gamma,)
        absmean.defvjp(_absmean_fwd, _absmean_bwd)

        def layernorm(x, w, b, eps=LN_EPS):
            mu = jnp.mean(x, axis=-1, keepdims=True)
            var = jnp.mean((x - mu) ** 2, axis=-1, keepdims=True)
            return (x - mu) * jax.lax.rsqrt(var + eps) * w + b
        key = jax.random.key(seed)
        k1, k2, k3 = jax.random.split(key, 3)
        d, h = (256, 1024)
        B, T = (8, 512)
        return {'x': jax.random.normal(k1, (B, T, d), jnp.float32), 'W_fc': jax.random.normal(k2, (h, d), jnp.float32), 'ln_w': jnp.ones((h,), jnp.float32), 'ln_b': jnp.zeros((h,), jnp.float32), 'W_proj': jax.random.normal(k3, (d, h), jnp.float32)}
    _L0_ffn_all = _L0_ffn_setup()
    _L0_ffn_in = {k: v for k, v in _L0_ffn_all.items() if k in ('W_fc', 'ln_w', 'ln_b', 'W_proj')}
    del _L0_ffn_all
    return {'x': x, 'ctx_1024': ctx_1024, 'L0_xattn_W_attn': _L0_xattn_in['W_attn'], 'L0_xattn_b_attn': _L0_xattn_in['b_attn'], 'L0_xattn_W_proj': _L0_xattn_in['W_proj'], 'L0_xattn_b_proj': _L0_xattn_in['b_proj'], 'L0_ffn_W_fc': _L0_ffn_in['W_fc'], 'L0_ffn_ln_w': _L0_ffn_in['ln_w'], 'L0_ffn_ln_b': _L0_ffn_in['ln_b'], 'L0_ffn_W_proj': _L0_ffn_in['W_proj']}

def reference(x, ctx_1024, L0_xattn_W_attn, L0_xattn_b_attn, L0_xattn_W_proj, L0_xattn_b_proj, L0_ffn_W_fc, L0_ffn_ln_w, L0_ffn_ln_b, L0_ffn_W_proj):
    import jax
    import jax.numpy as jnp

    def _L0_xattn_ref(x, ext_mem, W_attn, b_attn, W_proj, b_proj):
        import jax, jax.numpy as jnp
        import numpy as np
        EMBED_DIM = 256
        N_HEAD = 16
        HEAD_DIM = EMBED_DIM // N_HEAD
        B, T, C = x.shape
        qkv = x @ W_attn + b_attn
        q, k, v = jnp.split(qkv, 3, axis=2)
        to_heads = lambda t: t.reshape(B, -1, N_HEAD, HEAD_DIM).transpose(0, 2, 1, 3)
        q, k, v = (to_heads(q), to_heads(k), to_heads(v))
        mem_k = to_heads(ext_mem)
        k = jnp.concatenate([mem_k, k], axis=2)
        v = jnp.concatenate([mem_k, v], axis=2)
        mem_len = k.shape[2] - T
        att = jnp.einsum('bhtd,bhsd->bhts', q, k) * (1.0 / np.sqrt(HEAD_DIM))
        causal = jnp.tril(jnp.ones((T, T), dtype=bool))
        full_mask = jnp.concatenate([jnp.ones((T, mem_len), dtype=bool), causal], axis=1)
        att = jnp.where(full_mask[None, None], att, -jnp.inf)
        att = jax.nn.softmax(att, axis=-1)
        y = jnp.einsum('bhts,bhsd->bhtd', att, v)
        y = y.transpose(0, 2, 1, 3).reshape(B, T, C)
        return y @ W_proj + b_proj

    def _L0_ffn_ref(x, W_fc, ln_w, ln_b, W_proj):
        import jax, jax.numpy as jnp
        import numpy as np
        EPS = 1e-06
        LN_EPS = 1e-05

        def _absmean_core(W):
            gamma = jnp.mean(jnp.abs(W)) + EPS
            Ws = W / gamma
            Wq = jnp.sign(Ws) * jnp.minimum(jnp.round(jnp.abs(Ws)), 1.0)
            return (Wq, gamma)

        @jax.custom_vjp
        def absmean(W):
            return _absmean_core(W)[0]

        def _absmean_fwd(W):
            Wq, gamma = _absmean_core(W)
            return (Wq, gamma)

        def _absmean_bwd(gamma, g):
            return (g / gamma,)
        absmean.defvjp(_absmean_fwd, _absmean_bwd)

        def layernorm(x, w, b, eps=LN_EPS):
            mu = jnp.mean(x, axis=-1, keepdims=True)
            var = jnp.mean((x - mu) ** 2, axis=-1, keepdims=True)
            return (x - mu) * jax.lax.rsqrt(var + eps) * w + b
        h = jnp.einsum('btd,hd->bth', x, absmean(W_fc))
        h = jax.nn.gelu(h, approximate=False)
        h = layernorm(h, ln_w, ln_b)
        return jnp.einsum('bth,dh->btd', h, absmean(W_proj))
    x = x + _L0_xattn_ref(_layernorm(x, axis=-1), ctx_1024, L0_xattn_W_attn, L0_xattn_b_attn, L0_xattn_W_proj, L0_xattn_b_proj)
    x = x + _L0_ffn_ref(_layernorm(x, axis=-1), L0_ffn_W_fc, L0_ffn_ln_w, L0_ffn_ln_b, L0_ffn_W_proj)
    return x

_drawn_inputs = setup_inputs


def setup_inputs(seed=0):
    import zlib

    import numpy as np

    out = dict(_drawn_inputs(seed))
    spreads = {'L0_ffn_ln_w': (1.0, 0.2), 'L0_ffn_ln_b': (0.0, 0.1)}
    factors = {'L0_xattn_b_attn': 3.191}
    for name, (base, spread) in spreads.items():
        noise = np.random.default_rng([zlib.crc32(name.encode()), seed]).standard_normal(out[name].shape)
        drawn = base * np.exp(spread * noise) if base else spread * noise
        out[name] = jnp.asarray(drawn.astype(out[name].dtype))
    for name, factor in factors.items():
        out[name] = (out[name] * factor).astype(out[name].dtype)
    return out
```

```python
from contextlib import ExitStack

import concourse.bass as bass
from concourse import mybir

F32 = mybir.dt.float32
BF16 = mybir.dt.bfloat16
F16 = mybir.dt.float16
ALU = mybir.AluOpType
ACT = mybir.ActivationFunctionType
AX = mybir.AxisListType

B, T, D = 2, 1024, 256
MEM = 77
NH, HD = 16, 16
H = 1024
P = 128
KD = D // P
HG = 4
GB = NH // HG
NG = B * GB
S = MEM + T
KB = -(-S // P)
LAST = S - (KB - 1) * P
SP = 1104
CH = 512
NC = B * T // CH
CB = T // CH
TT = CH // P
HJ = H // P
LN_EPS = 1e-5
TERN_EPS = 1e-6
BIG = -1e30
LOWEST = -3.0e38
PAIRS = [(0, 0), (0, 1), (0, 2), (1, 0), (1, 1), (2, 0)]
KR = len(PAIRS) * HD
KM = KR + 3

BLOCKS = [[0, 3, 1, 2, 4], [0, 7, 1, 6, 2, 5, 3, 4, 8]]
STEPS = []
for _c in range(CB):
    for _j in BLOCKS[_c]:
        _lo = max(_c * CH, _j * P - MEM)
        STEPS.append((_c, _j, _lo - _c * CH, _lo, (_c + 1) * CH - _lo))
    assert sorted(BLOCKS[_c]) == [j for j in range(KB) if j * P - MEM < (_c + 1) * CH]
NS = len(STEPS)
CEND = [max(s for s, st in enumerate(STEPS) if st[0] == c) for c in range(CB)]
DIAG = []
for _c, _j, _col, _tok, _w in STEPS:
    _a, _b = max(_tok, _j * P - MEM), min(_tok + _w, _j * P - MEM + P)
    DIAG.append((_a - _tok, _b - _a) if _b > _a else None)
NDIAG = sum(d is not None for d in DIAG)
UNITS = []
for _c in range(CB):
    _u = []
    for _i in range(_c * TT, (_c + 1) * TT):
        _n = MEM + P * (_i + 1)
        _u += [(_i, _s, _s * CH, min(CH, _n - _s * CH)) for _s in range(-(-_n // CH))]
    _u.sort(key=lambda u: u[3])
    _steps = sorted((n for n, st in enumerate(STEPS) if st[0] == _c), key=lambda n: (-STEPS[n][4], n))
    _steps.remove(CEND[_c])
    _mine = dict(zip(_steps, _u[1:])) | {CEND[_c]: _u[0]}
    UNITS += [_mine[n] for n in sorted(_mine)]
NU = len(UNITS)
assert NU == NS
UA = sum(u[0] < TT for u in UNITS)
MSLOTS = max(u[1] for u in UNITS) + 1
LOADS = len(PAIRS)
PRIME, DMA_PRIME = 1, 16
PB = 4
LAG = 2


def build(nc, x, ctx_in, w_attn, b_attn, w_proj, b_proj, w_fc, ln_w, ln_b, w_out, out):
    q_scr = nc.dram_tensor("q_scr", [NG, HG, HD, 3, T], BF16).ap()
    k_scr = nc.dram_tensor("k_scr", [NG, HG, HD, 3, SP], BF16).ap()
    v_scr = nc.dram_tensor("v_scr", [NG, KB * P, 2 * HG * HD], F32).ap()
    y_scr = nc.dram_tensor("y_scr", [B, GB, P, T], F32).ap()
    m_scr = nc.dram_tensor("m_scr", [3, HG * TT, P], BF16).ap()
    q_st = q_scr.rearrange("(m g) h d a t -> m (g h d) a t", g=2)
    k_st = k_scr.rearrange("(m g) h d a t -> m (g h d) a t", g=2)
    v_st_view = v_scr.rearrange("(b g) s d -> b s g d", g=GB)
    x_ch = x.rearrange("b (c i p) d -> (b c) p i d", i=TT, p=P)
    out_ch = out.rearrange("b (c i p) d -> (b c) p i d", i=TT, p=P)

    with ExitStack() as es:
        def sb(name, shape, dt=F32):
            return es.enter_context(nc.sbuf_tensor(name, shape, dt))

        def sem(name):
            return es.enter_context(nc.semaphore(name))

        def sems(name, n):
            return [sem(f"{name}{i}") for i in range(n)]

        ps = es.enter_context(nc.psum_tensor("ps", [P, 8, CH], F32))

        ident = sb("ident", [P, P])
        identh = sb("identh", [P, P], BF16)
        identt = sb("identt", [P, P], F16)
        ones = sb("ones", [P, P])
        mean_w = sb("mean_w", [P, P])
        nhalf = sb("nhalf", [P, TT])
        wqkv = sb("wqkv", [P, KD, 3 * D])
        wpr = sb("wpr", [P, KD, D])
        bqk = sb("bqk", [P, 2 * KD])
        bv = sb("bv", [P, D])
        bpr = sb("bpr", [P, D])
        lnw = sb("lnw", [P, HJ])
        lnb = sb("lnb", [P, HJ])
        fcT = sb("fcT", [P, KD, HJ, P], F16)
        w2 = sb("w2", [P, HJ, D + 2])
        c1 = sb("c1", [P, D])
        c2 = sb("c2", [P, D])
        gam = sb("gam", [P, 8])
        stq_m = [sb(f"stq_m{i}", [P, HG, T], BF16) for i in range(2)]
        stk_m = [sb(f"stk_m{i}", [P, HG, SP], BF16) for i in range(2)]
        stq_e = [sb(f"stq_e{i}", [P, HG, T], BF16) for i in range(2)]
        stk_e = [sb(f"stk_e{i}", [P, HG, SP], BF16) for i in range(2)]
        vst = [sb(f"vst{i}", [P, KB, HG, 2 * HD]) for i in range(2)]
        probs = [sb(f"probs{i}", [P, HG, CH]) for i in range(PB)]
        window = sb("window", [P, S], BF16)
        junk = [sb(f"junk{i}", [P, CH], BF16) for i in range(2)]
        mpart = [sb(f"mpart{i}", [P, HG, TT, MSLOTS]) for i in range(CB)]
        negm = sb("negm", [P, HG * TT])
        mres = sb("mres", [P, HG * TT])
        mparts = sb("mparts", [P, 3, HG * TT], BF16)
        mrows = sb("mrows", [3 * HG * TT, P], BF16)
        ystage = [sb(f"ystage{i}", [P, CH]) for i in range(CB)]
        raw_fc = stk_m[0][:, :, :].rearrange("p h s -> p (h s)")[:, 0:2 * HJ * D].bitcast(F32)
        raw_fc = raw_fc.rearrange("p (j d) -> p j d", d=D)
        raw_out = stk_m[1][:, :, :].rearrange("p h s -> p (h s)")[:, 0:2 * KD * H].bitcast(F32)
        raw_out = raw_out.rearrange("p (k h) -> p k h", h=H)
        wT = stq_m[0][:, :, :].rearrange("p h s -> p (h s)")[:, 0:2 * HJ * D].bitcast(F32)
        wT = wT.rearrange("p (j d) -> p j d", d=D)
        lnb_wide = stq_m[1][:, :, :].rearrange("p h s -> p (h s)")[:, 0:2 * HJ * P].bitcast(F32)
        lnb_wide = lnb_wide.rearrange("p (j m) -> p j m", m=P)
        x_a = [sb(f"x_a{i}", [P, TT, D]) for i in range(2)]
        xn = sb("xn", [P, TT, D])
        xnT = sb("xnT", [P, KD, CH])
        stats = sb("stats", [P, TT, 6])
        mv = sb("mv", [P, TT, 2])
        ve = sb("ve", [P, TT])
        rs = sb("rs", [P, TT])
        parts = [sb(f"parts{i}", [P, 3, CH], BF16) for i in range(2)]
        resid = [sb(f"resid{i}", [P, CH]) for i in range(2)]
        vtile = [sb(f"vtile{i}", [P, NH, 2 * HD]) for i in range(2)]
        vctx = sb("vctx", [MEM, B, NH, 2 * HD])
        ctx_t = sb("ctx_t", [MEM, B, D])
        ctx_p = sb("ctx_p", [P, 3, B * KD, MEM], BF16)
        ctx_r = sb("ctx_r", [P, B * KD * MEM])
        rden = [sb(f"rden{i}", [P, NH]) for i in range(2)]

        def room(t, first, shape, dt=F32):
            v = t[:, :, :].rearrange("p a b -> p (a b)").bitcast(F32)
            a, b = shape
            words = a * b // (1 if dt == F32 else 2)
            v = v[:, first:first + words]
            return (v if dt == F32 else v.bitcast(dt)).rearrange("p (a b) -> p a b", b=b)

        yraw = room(stq_m[0], 0, (GB, CH))
        yn = room(stq_m[1], 0, (TT, D))
        ynT = room(stq_m[1], TT * D, (KD, CH))
        xb = room(stk_m[0], 0, (TT, D))
        x2 = room(stk_m[0], TT * D, (TT, D))
        x2c = room(stk_m[1], 0, (TT, D))
        o_t = room(stk_m[1], TT * D, (TT, D))
        hi = room(stq_e[1], 0, (KD, CH), F16)
        lo = room(stq_e[1], KD * CH // 2, (KD, CH), F16)
        g_lo = stk_e[0][:, :, :].rearrange("p h s -> p (h s)")[:, 0:HJ * CH].bitcast(F32)
        g_hi = stq_e[0][:, :, :].rearrange("p h s -> p (h s)")[:, 0:HJ * CH].bitcast(F32)
        gel = [(g_lo if j < HJ // 2 else g_hi)[:, (j % (HJ // 2)) * CH:(j % (HJ // 2) + 1) * CH] for j in range(HJ)]
        sq = probs
        tern_a = probs[0][:, :, :].rearrange("p h t -> p (h t)").bitcast(F16)[:, 0:HJ * D]
        tern_b = probs[1][:, :, :].rearrange("p h t -> p (h t)").bitcast(F16)
        tern_fcv = tern_b[:, 0:HJ * D].rearrange("p (j d) -> p j d", d=D)
        tern_outv = tern_b[:, HJ * D:2 * HJ * D].rearrange("p (k h) -> p k h", h=H)
        ssq2 = sb("ssq2", [P, CH])
        ssq = sb("ssq", [P, CH])
        fst = sb("fst", [P, 8])
        t1 = sb("t1", [P, D])

        fc_ld, wo_ld, small_ld, qkvw_ld = sem("fc_ld"), sem("wo_ld"), sem("small_ld"), sem("qkvw_ld")
        late_ld, ctx_ld = sem("late_ld"), sem("ctx_ld")
        dve_w, dve_a, dve_b, dve_c, pool_own = sem("dve_w"), sem("dve_a"), sem("dve_b"), sem("dve_c"), sem("pool_own")
        const_ready, ones_ready = sem("const_ready"), sem("ones_ready")
        abs_ready, gam_full = sem("abs_ready"), sem("gam_full")
        tern_ready, wt_full, wt_read = sem("tern_ready"), sem("wt_full"), sem("wt_read")
        w2_ready, cc_full, cc_read = sem("w2_ready"), sem("cc_full"), sem("cc_read")
        ctx_full, ctx_p1, ctx_p2, ctx_p3 = sem("ctx_full"), sem("ctx_p1"), sem("ctx_p2"), sem("ctx_p3")
        ctx_st, vctx_ready = sem("ctx_st"), sem("vctx_ready")
        x_ld = sems("x_ld", 2)
        ve_ready, rs_ready, xn_ready = sem("ve_ready"), sem("rs_ready"), sems("xn_ready", 2)
        xT_full, xT_evac = sem("xT_full"), sem("xT_evac")
        qk_full = sems("qk_full", 2)
        p1_ready, p2_ready, p3_ready = sems("p1_ready", 2), sems("p2_ready", 2), sems("p3_ready", 2)
        r_ready = sems("r_ready", 2)
        qk_st, v_full, v_ready, v_st = sems("qk_st", 2), sems("v_full", 2), sems("v_ready", 2), sems("v_st", 2)
        m_ld = sems("m_ld", 2)
        e_ld = sems("e_ld", 2)
        vs_ld = sems("vs_ld", 2)
        mx_full, mx_read = sems("mx_full", 2), sems("mx_read", 2)
        mp_ready, mt_full, mr_ready = sem("mp_ready"), sem("mt_full"), sem("mr_ready")
        mr_st, mr_ld = sem("mr_st"), sem("mr_ld")
        sc_full, pr_ready, sel_ready = sems("sc_full", 2), sems("pr_ready", 2), sems("sel_ready", 2)
        pv_done = sem("pv_done")
        y_ready, y_st = sems("y_ready", CB), sems("y_st", CB)
        c_ld, x3_ld, xb_ready = sem("c_ld"), sem("x3_ld"), sem("xb_ready")
        yt_full, yn_ready = sem("yt_full"), sems("yn_ready", 2)
        big_full, ynT_ready, hi_ready, lo_ready = sem("big_full"), sem("ynT_ready"), sem("hi_ready"), sem("lo_ready")
        pj_full, x2_ready, x2c_ready = sem("pj_full"), sems("x2_ready", 2), sem("x2c_ready")
        ve3, rs3, xn3 = sem("ve3"), sem("rs3"), sem("xn3")
        fc_full, gel_ready, sq_ready, ssq_ready = sem("fc_full"), sem("gel_ready"), sem("sq_ready"), sem("ssq_ready")
        fo_full, ve4, rs4 = sems("fo_full", 2), sem("ve4"), sem("rs4")
        o_ready, o_st = sems("o_ready", 2), sem("o_st")

        XT = ps[:, 0:2, :]
        QK = [ps[:, 2, :], ps[:, 3, :]]
        VV = [ps[:, 4, 0:D], ps[:, 5, 0:D]]
        CT = ps[:, 6, 0:B * KD * MEM]
        WT = ps[:, 7, :].bitcast(F16)
        SC = [ps[:, 0:2, :], ps[:, 2:4, :]]
        MX = [ps[:, 4, :], ps[:, 5, :]]
        ACC = ps[:, 6, :]
        MT = ps[0:3 * HG * TT, 7, 0:P // 2].bitcast(BF16)
        YT = [ps[:, 0, :], ps[:, 1, :]]
        BIGT = ps[:, 2:4, :]
        FC = [ps[:, 4, :], ps[:, 5, :]]
        FO = [ps[:, 6, 0:D + 2], ps[:, 7, 0:D + 2]]

        block = es.enter_context(nc.Block())

        def two_halves(i):
            return [(hf, 2 * i + hf) for hf in range(2)]

        def prime(eng, value, *signals):
            for signal in signals:
                eng.sem_inc(signal, value)

        def wait_apart(eng, signal, count):
            if not isinstance(count, int):
                count = eng.to_reg(count)
            eng.wait_ge(const_ready, 6)
            eng.wait_ge(signal, count)

        def wait_all(eng, *waits):
            waits = [(sig, count if isinstance(count, int) else eng.to_reg(count)) for sig, count in waits]
            for signal, count in waits:
                eng.wait_ge(signal, count)

        def occ(i, off):
            return i + off // 2

        @block.sync
        def _(sp):
            prime(sp, PRIME, *xn_ready, *sc_full, yt_full, xb_ready)
            sp.dma_start(raw_fc, w_fc.rearrange("(p j) d -> p j d", j=HJ)).then_inc(fc_ld, 16)
            sp.dma_start(raw_out, w_out.rearrange("(k p) h -> p k h", p=P)).then_inc(wo_ld, 16)
            sp.dma_start(lnw[:, :], ln_w.rearrange("(p j) -> p j", j=HJ)).then_inc(small_ld, 16)
            sp.dma_start(lnb[:, :], ln_b.rearrange("(p j) -> p j", j=HJ)).then_inc(small_ld, 16)
            for b in range(B):
                sp.dma_start(ctx_t[:, b, :], ctx_in[b]).then_inc(ctx_ld, 16)
            sp.dma_start(wqkv[:, :, :], w_attn.rearrange("(k p) n -> p k n", p=P)).then_inc(qkvw_ld, 16)
            sp.dma_start(bqk[:, :], b_attn[0:2 * D].rearrange("(m p) -> p m", p=P),
                         allow_slow_non_contiguous=True).then_inc(qkvw_ld, 16)
            sp.dma_start(bv[:, :], b_attn[2 * D:3 * D].partition_broadcast(P)).then_inc(qkvw_ld, 16)
            sp.dma_start(wpr[:, :, :], w_proj.rearrange("(k p) n -> p k n", p=P)).then_inc(late_ld, 16)
            sp.dma_start(bpr[:, :], b_proj.partition_broadcast(P)).then_inc(late_ld, 16)
            sp.wait_ge(vctx_ready, 2)
            for b in range(B):
                sp.dma_start(v_st_view[b, 0:MEM], vctx[:, b, :, :].rearrange("p (g h) d -> p g (h d)", g=GB))\
                    .then_inc(ctx_st, 16)
            for a, part_ready in enumerate((ctx_p1, ctx_p2, ctx_p3)):
                sp.wait_ge(part_ready, 1)
                sp.dma_start(k_st[:, :, a, 0:MEM].rearrange("m r t -> r m t"), ctx_p[:, a, :, :]).then_inc(ctx_st, 16)
            with sp.Fori(0, B) as i:
                for hf in range(CB):
                    sp.wait_ge(xn_ready[hf], PRIME + TT * i)
                    sp.dma_start(x_a[hf][:, :, :], x_ch[2 * i + hf]).then_inc(x_ld[hf], 16)
                for hf in range(CB):
                    n = 2 * i + hf
                    for m in range(2 * KD):
                        pb = m % 2
                        sp.wait_ge(p3_ready[pb], PRIME + 2 * n + m // 2 + 1)
                        dst = (q_st if m < KD else k_st)[2 * i + m % KD]
                        off = CH * hf + (0 if m < KD else MEM)
                        sp.dma_start(dst[:, :, off:off + CH], parts[pb][:, :, :]).then_inc(qk_st[pb], 16)
                    for tt in range(TT):
                        vb, row = tt % 2, MEM + CH * hf + P * tt
                        sp.wait_ge(v_ready[vb], PRIME + 2 * n + tt // 2 + 1)
                        sp.dma_start(v_st_view[i, row:row + P], vtile[vb][:, :, :].rearrange("p (g h) d -> p g (h d)", g=GB))\
                            .then_inc(v_st[vb], 16)

            for pb in range(2):
                sp.wait_ge(qk_st[pb], DMA_PRIME + 16 * 2 * NC)
                sp.wait_ge(v_st[pb], DMA_PRIME + 16 * 2 * NC)
            sp.wait_ge(ctx_st, 16 * (B + 3))

            def load_stack(q_dst, k_dst, g, done):
                for r, (qa, ka) in enumerate(PAIRS):
                    rows = slice(r * HD, (r + 1) * HD)
                    sp.dma_start(q_dst[rows, :, :], q_scr[g, :, :, qa, :].rearrange("h d t -> d h t")).then_inc(done, 16)
                    sp.dma_start(k_dst[rows, :, 0:S], k_scr[g, :, :, ka, 0:S].rearrange("h d t -> d h t"))\
                        .then_inc(done, 16)

            def load_values(v_dst, g, done):
                sp.dma_start(v_dst[:, 0:KB - 1, :, :].rearrange("p j h d -> p j (h d)"),
                             v_scr[g, 0:(KB - 1) * P, :].rearrange("(j p) d -> p j d", p=P)).then_inc(done, 16)
                sp.dma_start(v_dst[0:LAST, KB - 1, :, :].rearrange("p h d -> p (h d)"),
                             v_scr[g, (KB - 1) * P:S, :]).then_inc(done, 16)

            def copy_stack(par, loads, *before):
                wait_all(sp, *before, (m_ld[par], 16 * 2 * LOADS * loads))
                sp.dma_start(stq_e[par][0:KR, :, :], stq_m[par][0:KR, :, :]).then_inc(e_ld[par], 16)
                sp.dma_start(stk_e[par][0:KR, :, 0:S], stk_m[par][0:KR, :, 0:S]).then_inc(e_ld[par], 16)

            def place_max_rows(par, c, q):
                sp.wait_ge(mr_ready, q + 1)
                sp.dma_start(m_scr.rearrange("a r t -> (a r) t"), mrows[:, :]).then_inc(mr_st, 16)
                sp.wait_ge(mr_st, 16 * q + 16)
                sp.dma_start(stq_e[par][KR:KM, :, c * CH:(c + 1) * CH],
                             m_scr.rearrange("a (h i) t -> a h (i t)", h=HG)).then_inc(mr_ld, 16)

            sp.wait_ge(w2_ready, 1)
            sp.wait_ge(cc_full, 2)
            load_stack(stq_m[0], stk_m[0], 0, m_ld[0])
            load_stack(stq_m[1], stk_m[1], 1, m_ld[1])
            load_values(vst[0], 0, vs_ld[0])
            copy_stack(0, 1)
            place_max_rows(0, 0, 0)

            def slot(i, u, more_m, more_e):
                g = 2 * i + u
                place_max_rows(u, 1, 2 * g + 1)
                if more_e:
                    copy_stack(1 - u, occ(i, u + 1) + 1, (sc_full[1], PRIME + NS * g))
                if more_m:
                    wait_all(sp, (mx_full[1], 2 * NU * (g + 1)), (e_ld[u], 16 * 2 * (i + 1)))
                    load_stack(stq_m[u], stk_m[u], g + 2, m_ld[u])
                if more_e:
                    sp.wait_ge(pv_done, PB + NS * g)
                    load_values(vst[1 - u], g + 1, vs_ld[1 - u])
                sp.wait_ge(y_ready[0], PRIME + g + 1)
                sp.dma_start(y_scr[g // GB, g % GB, :, 0:CH], ystage[0][:, :]).then_inc(y_st[0], 16)
                if more_e:
                    place_max_rows(1 - u, 0, 2 * g + 2)
                sp.wait_ge(y_ready[1], PRIME + g + 1)
                sp.dma_start(y_scr[g // GB, g % GB, :, CH:T], ystage[1][:, :]).then_inc(y_st[1], 16)

            with sp.Fori(0, NG // 2 - 1) as i:
                slot(i, 0, True, True)
                slot(i, 1, True, True)
            slot(NG // 2 - 1, 0, False, True)
            slot(NG // 2 - 1, 1, False, False)

            for c in range(CB):
                sp.wait_ge(y_st[c], DMA_PRIME + 16 * NG)
            y_ch = y_scr.rearrange("b g p (c t) -> b c p g t", c=CB)
            with sp.Fori(0, NC) as n:
                sp.wait_ge(yt_full, PRIME + TT * n)
                sp.dma_start(yraw[:, :, :], y_ch[n // CB, n % CB]).then_inc(c_ld, 16)
                sp.wait_ge(xb_ready, PRIME + n)
                sp.dma_start(x_a[0][:, :, :], x_ch[n]).then_inc(x3_ld, 16)
                for k in range(2):
                    sp.wait_ge(o_ready[k], PRIME + 2 * n + 2)
                sp.dma_start(out_ch[n], o_t[:, :, :]).then_inc(o_st, 16)
            sp.wait_ge(o_st, DMA_PRIME + 16 * NC)

        @block.gpsimd
        def _(pool):
            prime(pool, PRIME, *x2_ready, *o_ready)
            for t in (ident, identh, identt):
                pool.memset(t[:, :], 0.0).then_inc(pool_own, 1)
            pool.memset(window[:, :], 0.0).then_inc(pool_own, 1)
            pool.wait_ge(pool_own, 4)
            for t in (ident, identh, identt):
                pool.affine_select(out=t[:, :], in_=t[:, :], compare_op=ALU.not_equal, fill=1.0, base=0,
                                   pattern=[[-1, P]], channel_multiplier=1).then_inc(const_ready, 1)
            pool.affine_select(out=window[:, S - P:S], in_=window[:, S - P:S], compare_op=ALU.is_ge, fill=BIG,
                               base=0, pattern=[[-1, P]], channel_multiplier=1).then_inc(const_ready, 1)
            pool.memset(ones[:, :], 1.0).then_inc(const_ready, 1)
            pool.memset(nhalf[:, :], -0.5).then_inc(pool_own, 1)
            pool.memset(mean_w[:, :], 1.0 / (H * D)).then_inc(const_ready, 1)
            for par in range(2):
                pool.memset(vtile[par][:, :, HD:2 * HD], 1.0).then_inc(ones_ready, 1)
            pool.memset(vctx[:, :, :, HD:2 * HD], 1.0).then_inc(vctx_ready, 1)
            for c in range(CB):
                pool.memset(mpart[c][:, :, :, :], LOWEST).then_inc(ones_ready, 1)
            pool.memset(w2[:, :, D:D + 2], 1.0).then_inc(ones_ready, 1)
            pool.wait_ge(pool_own, 5)
            pool.wait_ge(ctx_p2, 1)
            pool.tensor_tensor(ctx_p[:, 2, :, :].rearrange("p m t -> p (m t)"), ctx_r[:, :],
                               ctx_p[:, 1, :, :].rearrange("p m t -> p (m t)"), ALU.subtract).then_inc(ctx_p3, 1)
            with pool.Fori(0, B) as i:
                for hf in range(CB):
                    n = 2 * i + hf
                    pool.wait_ge(ve_ready, n + 1)
                    pool.tensor_tensor(rs[:, :], ve[:, :], nhalf[:, :], ALU.pow).then_inc(rs_ready, 1)
                    for m in range(2 * KD):
                        pb = m % 2
                        pool.wait_ge(p2_ready[pb], 2 * n + m // 2 + 1)
                        pool.tensor_tensor(parts[pb][:, 2, :], resid[pb][:, :], parts[pb][:, 1, :],
                                           ALU.subtract).then_inc(p3_ready[pb], 1)

            def slot(i, u):
                g = 2 * i + u
                for s, (c, j, col, tok, w) in enumerate(STEPS):
                    if DIAG[s] is None:
                        continue
                    a, dw = DIAG[s]
                    rows = P if j < KB - 1 else LAST
                    for k in range(2):
                        wait_apart(pool, pr_ready[k], PRIME + NS * g + s + 1)
                        part = probs[(NS * u + s) % PB][0:rows, 2 * k:2 * k + 2, a:a + dw]
                        pool.affine_select(out=part, in_=part, compare_op=ALU.is_ge, fill=0.0,
                                           base=tok + a + MEM - P * j, pattern=[[0, 2], [1, dw]],
                                           channel_multiplier=-1).then_inc(sel_ready[k], 1)

            with pool.Fori(0, NG // 2) as i:
                slot(i, 0)
                slot(i, 1)

            pool.wait_ge(late_ld, 32)
            pool.wait_ge(cc_read, 2)
            with pool.Fori(0, NC) as n:
                pool.wait_ge(x3_ld, 16 * n + 16)
                pool.wait_ge(x2_ready[0], PRIME + 2 * n)
                pool.wait_ge(x2_ready[1], PRIME + 2 * n)
                pool.tensor_tensor(xb[:, :, :], x_a[0][:, :, :],
                                   bpr[:, :].rearrange("p (o d) -> p o d", o=1).to_broadcast([P, TT, D]),
                                   ALU.add).then_inc(xb_ready, 1)
                pool.wait_ge(ve3, n + 1)
                pool.tensor_tensor(rs[:, :], ve[:, :], nhalf[:, :], ALU.pow).then_inc(rs3, 1)
                pool.wait_ge(o_ready[0], PRIME + 2 * n)
                pool.wait_ge(o_ready[1], PRIME + 2 * n)
                pool.tensor_tensor(x2c[:, :, :], x2[:, :, :],
                                   c2[:, :].rearrange("p (o d) -> p o d", o=1).to_broadcast([P, TT, D]),
                                   ALU.add).then_inc(x2c_ready, 1)
                for tt in range(TT):
                    pool.wait_ge(ve4, TT * n + tt + 1)
                    pool.tensor_tensor(fst[:, 6:7], fst[:, 5:6], nhalf[:, 0:1], ALU.pow).then_inc(rs4, 1)

        @block.scalar
        def _(act):
            prime(act, PRIME, *v_full, ssq_ready)
            prime(act, PB, pv_done)
            prime(act, DMA_PRIME, *qk_st, *y_st)
            act.wait_ge(ctx_full, 1)
            act.activation(ctx_p[:, 0, :, :].rearrange("p m t -> p (m t)"), CT, ACT.Copy).then_inc(ctx_p1, 1)
            for r in range(2 * KD):
                act.wait_ge(wt_full, r + 1)
                k = r % KD
                src = WT.rearrange("p (j c) -> p j c", c=P)
                dst = fcT[:, k, :, :] if r < KD else wT[:, :, k * P:(k + 1) * P]
                act.activation(dst, src, ACT.Copy).then_inc(wt_read, 1)
            for which, dst in enumerate((c1, c2)):
                act.wait_ge(cc_full, which + 1)
                act.activation(dst[:, :], VV[which], ACT.Copy).then_inc(cc_read, 1)
            act.wait_ge(qkvw_ld, 48)
            with act.Fori(0, B) as i:
                for hf in range(CB):
                    n = 2 * i + hf
                    for k in range(KD):
                        if k == 0:
                            act.wait_ge(xT_full, PRIME + n + 1)
                            act.wait_ge(v_full[1], PRIME + 2 * n)
                        act.activation(xnT[:, k, :], XT[:, k, :], ACT.Copy).then_inc(xT_evac, 1)
                    for m in range(2 * KD):
                        pb, use = m % 2, 2 * n + m // 2
                        act.wait_ge(qk_full[pb], use + 1)
                        act.wait_ge(qk_st[pb], DMA_PRIME + 16 * use)
                        act.activation(parts[pb][:, 0, :], QK[pb], ACT.Identity, bias=bqk[:, m:m + 1])\
                            .then_inc(p1_ready[pb], 1)

            def slot(i, u):
                g = 2 * i + u

                def save(c):
                    act.wait_ge(pv_done, PB + NS * g + CEND[c] + 1)
                    act.wait_ge(y_st[c], DMA_PRIME + 16 * g)
                    act.activation(ystage[c][:, :], ACC, ACT.Copy).then_inc(y_ready[c], 1)

                for s, (c, j, col, tok, w) in enumerate(STEPS):
                    rows = P if j < KB - 1 else LAST
                    for k in range(2):
                        act.wait_ge(sc_full[k], PRIME + NS * g + s + 1)
                        act.wait_ge(pv_done, NS * g + s + 1)
                        act.activation(probs[(NS * u + s) % PB][0:rows, 2 * k:2 * k + 2, 0:w], SC[k][0:rows, :, 0:w],
                                       ACT.Exp, scale=HD ** -0.5).then_inc(pr_ready[k], 1)
                    if s == CEND[0] + LAG:
                        save(0)
                save(1)

            with act.Fori(0, NG // 2) as i:
                slot(i, 0)
                slot(i, 1)

            with act.Fori(0, NC) as n:
                act.wait_ge(big_full, 2 * n + 1)
                for k in range(KD):
                    act.activation(ynT[:, k, :], BIGT[:, k, :], ACT.Copy).then_inc(ynT_ready, 1)
                act.wait_ge(big_full, 2 * n + 2)
                for k in range(KD):
                    act.activation(hi[:, k, :], BIGT[:, k, :], ACT.Copy).then_inc(hi_ready, 1)
                for j in range(HJ):
                    act.wait_ge(fc_full, HJ * n + j + 1)
                    act.activation(gel[j], FC[j % 2], ACT.Gelu).then_inc(gel_ready, 1)
                act.wait_ge(ssq_ready, PRIME + n)
                for j in range(HJ):
                    act.wait_ge(gel_ready, HJ * n + j + 1)
                    act.activation(sq[j // HG][:, j % HG, :], gel[j], ACT.Square).then_inc(sq_ready, 1)

        @block.vector
        def _(dve):
            prime(dve, PRIME, xT_full, *p3_ready, x2c_ready, xn3)
            prime(dve, DMA_PRIME, *v_st, o_st)
            own = [0]

            def chain(ins, signal=dve_w):
                own[0] += 1
                ins.then_inc(signal, 1)
                dve.wait_ge(signal, own[0])

            for par in range(2):
                dve.memset(stk_e[par][KR:KM, :, :], 1.0).then_inc(ones_ready, 1)
            dve.wait_ge(ctx_ld, 16 * B)
            dve.tensor_copy(vctx[:, :, :, 0:HD], ctx_t[:, :, :].rearrange("p b (h d) -> p b h d", d=HD))\
                .then_inc(vctx_ready, 1)
            dve.wait_ge(ctx_p1, 1)
            flat = [ctx_p[:, a, :, :].rearrange("p m t -> p (m t)") for a in range(3)]
            chain(dve.tensor_tensor(ctx_r[:, :], CT, flat[0], ALU.subtract))
            dve.tensor_copy(flat[1], ctx_r[:, :]).then_inc(ctx_p2, 1)
            dve.wait_ge(fc_ld, 16)
            dve.tensor_reduce(gam[:, 0:1], raw_fc, AX.XY, ALU.add, apply_absolute_value=True).then_inc(abs_ready, 1)
            dve.wait_ge(wo_ld, 16)
            dve.tensor_reduce(gam[:, 1:2], raw_out, AX.XY, ALU.add, apply_absolute_value=True).then_inc(abs_ready, 1)
            dve.wait_ge(gam_full, 1)
            chain(dve.tensor_scalar(gam[:, 2:4], VV[0][:, 0:2], TERN_EPS, 0.5, ALU.add, ALU.mult))
            chain(dve.tensor_scalar(gam[:, 4:6], gam[:, 2:4], -1.0, None, ALU.mult))
            for which, (raw, dst) in enumerate(((raw_fc, tern_fcv), (raw_out, tern_outv))):
                r2 = raw.rearrange("p a b -> p (a b)")
                chain(dve.tensor_scalar(tern_a, r2, gam[:, 4 + which:5 + which], None, ALU.is_lt))
                dve.scalar_tensor_tensor(dst.rearrange("p a b -> p (a b)"), r2, gam[:, 2 + which:3 + which], tern_a,
                                         ALU.is_gt, ALU.subtract).then_inc(tern_ready, 1)
                dve.wait_ge(tern_ready, which + 1)
            dve.wait_ge(small_ld, 32)
            dve.tensor_copy(lnb_wide, lnb[:, :].rearrange("p (j o) -> p j o", o=1).to_broadcast([P, HJ, P]))\
                .then_inc(dve_w, 1)
            own[0] += 1
            dve.wait_ge(wt_read, 2 * KD)
            for j in range(HJ):
                ins = dve.tensor_scalar(w2[:, j, 0:D], wT[:, j, :], lnw[:, j:j + 1], None, ALU.mult)
            ins.then_inc(w2_ready, 1)

            dve.wait_ge(qkvw_ld, 48)
            dve.wait_ge(ones_ready, 7)
            per_chunk = 2 * TT
            with dve.Fori(0, B) as i:
                for hf in range(CB):
                    n = 2 * i + hf
                    dve.wait_ge(x_ld[hf], 16 * i + 16)
                    for tt in range(TT):
                        dve.bn_stats(stats[:, tt, :], x_a[hf][:, tt, :]).then_inc(dve_a, 1)
                    wait_apart(dve, dve_a, per_chunk * n + TT)
                    for tt in range(TT):
                        dve.bn_aggr(mv[:, tt, :], stats[:, tt, :]).then_inc(dve_a, 1)
                    dve.wait_ge(dve_a, per_chunk * n + 2 * TT)
                    dve.tensor_scalar(ve[:, :], mv[:, :, 1], LN_EPS, None, ALU.add).then_inc(ve_ready, 1)
                    dve.wait_ge(rs_ready, n + 1)
                    dve.wait_ge(xT_full, PRIME + n)
                    for tt in range(TT):
                        dve.tensor_scalar(xn[:, tt, :], x_a[hf][:, tt, :], mv[:, tt, 0:1], rs[:, tt:tt + 1],
                                                ALU.subtract, ALU.mult).then_inc(xn_ready[hf], 1)
                    for m in range(2 * KD):
                        pb, use = m % 2, 2 * n + m // 2
                        dve.wait_ge(p1_ready[pb], use + 1)
                        dve.wait_ge(p3_ready[pb], PRIME + use)
                        dve.scalar_tensor_tensor(resid[pb][:, :], QK[pb], bqk[:, m:m + 1], parts[pb][:, 0, :],
                                                 ALU.add, ALU.subtract).then_inc(r_ready[pb], 1)
                        dve.wait_ge(r_ready[pb], PRIME + use + 1)
                        dve.tensor_copy(parts[pb][:, 1, :], resid[pb][:, :]).then_inc(p2_ready[pb], 1)
                    for tt in range(TT):
                        vb, use = tt % 2, 2 * n + tt // 2
                        dve.wait_ge(v_full[vb], PRIME + use + 1)
                        dve.wait_ge(v_st[vb], DMA_PRIME + 16 * use)
                        dve.tensor_tensor(vtile[vb][:, :, 0:HD], VV[vb].rearrange("p (h d) -> p h d", d=HD),
                                          bv[:, :].rearrange("p (h d) -> p h d", d=HD), ALU.add)\
                            .then_inc(v_ready[vb], 1)

            def unit(G, nu):
                qi, slot_, key, w = UNITS[nu]
                c, ti = qi // TT, qi % TT
                start = S - (MEM + P * (qi + 1)) + key
                for h in range(HG):
                    use = 2 * NU * G + 2 * nu + h // 2
                    wait_apart(dve, mx_full[h % 2], use + 1)
                    dve.tensor_tensor_reduce(junk[h % 2][:, 0:w], MX[h % 2][:, 0:w], window[:, start:start + w], 1.0, LOWEST,
                                             ALU.add, ALU.max, mpart[c][:, h, ti, slot_:slot_ + 1])\
                        .then_inc(mx_read[h % 2], 1)

            def split_max(G, c):
                q = CB * G + c
                done = 2 * NU * G + 2 * (UA if c == 0 else NU)
                dve.wait_ge(mx_read[0], done)
                dve.wait_ge(mx_read[1], done)
                dve.tensor_reduce(negm[:, :], mpart[c][:, :, :, :], AX.X, ALU.max, negate=True).then_inc(dve_b, 1)
                dve.wait_ge(dve_b, 4 * q + 1)
                dve.wait_ge(mt_full, q)
                dve.tensor_copy(mparts[:, 0, :], negm[:, :]).then_inc(dve_b, 1)
                dve.wait_ge(dve_b, 4 * q + 2)
                dve.tensor_tensor(mres[:, :], negm[:, :], mparts[:, 0, :], ALU.subtract).then_inc(dve_b, 1)
                dve.wait_ge(dve_b, 4 * q + 3)
                dve.tensor_copy(mparts[:, 1, :], mres[:, :]).then_inc(dve_b, 1)
                dve.wait_ge(dve_b, 4 * q + 4)
                dve.tensor_tensor(mparts[:, 2, :], mres[:, :], mparts[:, 1, :], ALU.subtract).then_inc(mp_ready, 1)

            def rows_out(q):
                dve.wait_ge(mt_full, q + 1)
                dve.wait_ge(mr_st, 16 * q)
                dve.tensor_copy(mrows[:, :], MT).then_inc(mr_ready, 1)

            def max_pass(G, first_rows):
                for nu in range(NU):
                    unit(G, nu)
                    if nu == 0 and first_rows is not None:
                        rows_out(first_rows)
                    if nu == UA - 1:
                        split_max(G, 0)
                    if nu == UA + 1:
                        rows_out(CB * G)
                split_max(G, 1)

            dve.wait_ge(const_ready, 6)
            dve.wait_ge(ones_ready, 7)
            max_pass(0, None)
            with dve.Fori(0, NG // 2 - 1) as i:
                for u in range(2):
                    max_pass(2 * i + u + 1, CB * (2 * i + u) + 1)
            max_pass(NG - 1, CB * (NG - 2) + 1)
            rows_out(CB * (NG - 1) + 1)

            with dve.Fori(0, NC) as n:
                per_n = TT + 2 * TT + 1 + 5 * TT
                base = per_n * n
                cnt = [0]

                def mark(ins):
                    cnt[0] += 1
                    ins.then_inc(dve_c, 1)
                    return base + cnt[0]

                for tt in range(TT):
                    yb = tt % 2
                    dve.wait_ge(yt_full, PRIME + TT * n + tt + 1)
                    y4 = YT[yb].rearrange("p (h r) -> p h r", r=2 * HD)
                    dve.wait_ge(dve_c, mark(dve.reciprocal(rden[yb][:, :], y4[:, :, HD])))
                    dve.tensor_tensor(yn[:, tt, :].rearrange("p (h d) -> p h d", d=HD), y4[:, :, 0:HD],
                                      rden[yb][:, :].rearrange("p (h o) -> p h o", o=1).to_broadcast([P, NH, HD]),
                                      ALU.mult).then_inc(yn_ready[yb], 1)
                dve.wait_ge(xb_ready, PRIME + n + 1)
                dve.wait_ge(x2c_ready, PRIME + n)
                for tt in range(TT):
                    yb = tt % 2
                    dve.wait_ge(pj_full, TT * n + tt + 1)
                    dve.tensor_tensor(x2[:, tt, :], FC[yb][:, 0:D], xb[:, tt, :], ALU.add).then_inc(x2_ready[yb], 1)
                    dve.wait_ge(x2_ready[yb], PRIME + 2 * n + tt // 2 + 1)
                    v = mark(dve.bn_stats(stats[:, tt, :], x2[:, tt, :]))
                    wait_apart(dve, dve_c, v)
                    last = mark(dve.bn_aggr(mv[:, tt, :], stats[:, tt, :]))
                dve.wait_ge(dve_c, last)
                dve.wait_ge(xn3, PRIME + TT * n)
                dve.tensor_scalar(ve[:, :], mv[:, :, 1], LN_EPS, None, ALU.add).then_inc(ve3, 1)
                dve.wait_ge(rs3, n + 1)
                for tt in range(TT):
                    dve.tensor_scalar(xn[:, tt, :], x2[:, tt, :], mv[:, tt, 0:1], rs[:, tt:tt + 1],
                                      ALU.subtract, ALU.mult).then_inc(xn3, 1)
                for k in range(KD):
                    dve.wait_ge(hi_ready, KD * n + k + 1)
                    dve.tensor_tensor(lo[:, k, :], BIGT[:, k, :], hi[:, k, :], ALU.subtract).then_inc(lo_ready, 1)
                dve.wait_ge(sq_ready, HJ * n + HJ // 2)
                mark(dve.tensor_reduce(ssq[:, :], sq[0][:, :, :].rearrange("p j t -> p t j"), AX.X, ALU.add))
                dve.wait_ge(sq_ready, HJ * n + HJ)
                dve.tensor_reduce(ssq2[:, :], sq[1][:, :, :].rearrange("p j t -> p t j"), AX.X, ALU.add)\
                    .then_inc(ssq_ready, 1)
                dve.wait_ge(x2c_ready, PRIME + n + 1)
                dve.wait_ge(o_st, DMA_PRIME + 16 * n)
                for tt in range(TT):
                    fb = tt % 2
                    dve.wait_ge(fo_full[fb], 2 * n + tt // 2 + 1)
                    v = mark(dve.tensor_scalar(fst[:, 0:2], FO[fb][:, D:D + 2], 1.0 / H, None, ALU.mult))
                    dve.wait_ge(dve_c, v)
                    v = mark(dve.tensor_tensor(fst[:, 2:3], fst[:, 0:1], fst[:, 0:1], ALU.mult))
                    mark(dve.tensor_scalar(fst[:, 3:4], fst[:, 0:1], -1.0, None, ALU.mult))
                    dve.wait_ge(dve_c, v)
                    v = mark(dve.tensor_tensor(fst[:, 4:5], fst[:, 1:2], fst[:, 2:3], ALU.subtract))
                    dve.wait_ge(dve_c, v)
                    dve.tensor_scalar(fst[:, 5:6], fst[:, 4:5], LN_EPS, None, ALU.add).then_inc(ve4, 1)
                    v = mark(dve.scalar_tensor_tensor(t1[:, :], c1[:, :], fst[:, 3:4], FO[fb][:, 0:D],
                                                      ALU.mult, ALU.add))
                    dve.wait_ge(dve_c, v)
                    dve.wait_ge(rs4, TT * n + tt + 1)
                    dve.scalar_tensor_tensor(o_t[:, tt, :], t1[:, :], fst[:, 6:7], x2c[:, tt, :],
                                             ALU.mult, ALU.add).then_inc(o_ready[fb], 1)
                    dve.wait_ge(o_ready[fb], PRIME + 2 * n + tt // 2 + 1)
                assert cnt[0] == per_n, (cnt[0], per_n)

        @block.tensor
        def _(pe):
            prime(pe, PRIME, xT_evac, *r_ready, *v_ready, *pr_ready, *y_ready, *yn_ready, lo_ready)
            pe.wait_ge(const_ready, 6)
            pe.wait_ge(ctx_ld, 16 * B)
            for b in range(B):
                for k in range(KD):
                    m = b * KD + k
                    ins = pe.transpose(CT[:, m * MEM:(m + 1) * MEM], ctx_t[:, b, k * P:(k + 1) * P],
                                       ident[0:MEM, 0:MEM])
            ins.then_inc(ctx_full, 1)
            pe.wait_ge(abs_ready, 2)
            pe.matmul(VV[0][:, 0:2], mean_w[:, :], gam[:, 0:2], start=True, stop=True).then_inc(gam_full, 1)
            for r in range(2 * KD):
                k = r % KD
                pe.wait_ge(tern_ready, 1 + (r >= KD))
                pe.wait_ge(wt_read, r)
                for j in range(HJ):
                    src = tern_fcv[:, j, k * P:(k + 1) * P] if r < KD else tern_outv[:, k, j:H:HJ]
                    ins = pe.transpose(WT[:, j * P:(j + 1) * P], src, identt[:, :])
                ins.then_inc(wt_full, 1)
            pe.wait_ge(w2_ready, 1)
            pe.wait_ge(dve_w, 6)
            for which in range(2):
                for j in range(HJ):
                    lhs, rhs = (ones[:, :], w2[:, j, 0:D]) if which == 0 else (lnb_wide[:, j, :], wT[:, j, :])
                    ins = pe.matmul(VV[which], lhs, rhs, start=(j == 0), stop=(j == HJ - 1))
                ins.then_inc(cc_full, 1)

            pe.wait_ge(qkvw_ld, 48)
            pe.wait_ge(cc_read, 2)
            with pe.Fori(0, B) as i:
                for hf in range(CB):
                    n = 2 * i + hf
                    pe.wait_ge(xT_evac, PRIME + KD * n)
                    for tt in range(TT):
                        pe.wait_ge(xn_ready[hf], PRIME + TT * i + tt + 1)
                        for k in range(KD):
                            ins = pe.transpose(XT[:, k, tt * P:(tt + 1) * P], xn[:, tt, k * P:(k + 1) * P], ident[:, :])
                    ins.then_inc(xT_full, 1)
                    pe.wait_ge(xT_evac, PRIME + KD * n + KD)
                    for m in range(2 * KD):
                        pb, use = m % 2, 2 * n + m // 2
                        pe.wait_ge(r_ready[pb], PRIME + use)
                        for k in range(KD):
                            ins = pe.matmul(QK[pb], wqkv[:, k, m * P:(m + 1) * P], xnT[:, k, :],
                                            start=(k == 0), stop=(k == KD - 1))
                        ins.then_inc(qk_full[pb], 1)
                    for tt in range(TT):
                        vb, use = tt % 2, 2 * n + tt // 2
                        pe.wait_ge(v_ready[vb], PRIME + use)
                        for k in range(KD):
                            ins = pe.matmul(VV[vb], xnT[:, k, tt * P:(tt + 1) * P], wqkv[:, k, 2 * D:3 * D],
                                            start=(k == 0), stop=(k == KD - 1))
                        ins.then_inc(v_full[vb], 1)

            def max_heads(G, par, nu, heads):
                qi, slot_, key, w = UNITS[nu]
                for h in heads:
                    use = 2 * NU * G + 2 * nu + h // 2
                    pe.wait_ge(mx_read[h % 2], use)
                    ins = pe.matmul(MX[h % 2][:, 0:w], stq_m[par][0:KR, h, qi * P:(qi + 1) * P],
                                    stk_m[par][0:KR, h, key:key + w], start=True, stop=True)
                    ins.then_inc(mx_full[h % 2], 1)

            def turn_rows(q):
                pe.wait_ge(mr_ready, q)
                wait_apart(pe, mp_ready, q + 1)
                pe.transpose(MT, mparts[:, :, :].rearrange("p a r -> p (a r)"), identh[:, :]).then_inc(mt_full, 1)

            def slot(i, u, more):
                g = 2 * i + u
                pe.wait_ge(e_ld[u], 16 * 2 * (i + 1))
                pe.wait_ge(vs_ld[u], 16 * 2 * (i + 1))
                if more:
                    pe.wait_ge(m_ld[1 - u], 16 * 2 * LOADS * (occ(i, u + 1) + 1))

                def pv(s):
                    c, j, col, tok, w = STEPS[s]
                    rows = P if j < KB - 1 else LAST
                    if j == 0:
                        pe.wait_ge(y_ready[1 - c], PRIME + g + c)
                    for h in range(HG):
                        if h % 2 == 0:
                            if DIAG[s] is None:
                                pe.wait_ge(pr_ready[h // 2], PRIME + NS * g + s + 1)
                            else:
                                done = sum(d is not None for d in DIAG[:s + 1])
                                pe.wait_ge(sel_ready[h // 2], NDIAG * g + done)
                        ins = pe.matmul(ACC[32 * h:32 * h + 32, col:col + w], vst[u][0:rows, j, h, :],
                                        probs[(NS * u + s) % PB][0:rows, h, 0:w], start=(j == 0),
                                        stop=(s == CEND[c]), skip_group_check=True)
                    ins.then_inc(pv_done, 1)

                for s, (c, j, col, tok, w) in enumerate(STEPS):
                    rows = P if j < KB - 1 else LAST
                    if j == 0:
                        pe.wait_ge(mr_ld, 16 * (CB * g + c + 1))
                    for k in range(2):
                        pe.wait_ge(pr_ready[k], PRIME + NS * g + s)
                        for h in (2 * k, 2 * k + 1):
                            ins = pe.matmul(SC[k][0:rows, h % 2, 0:w], stk_e[u][0:KM, h, j * P:j * P + rows],
                                            stq_e[u][0:KM, h, tok:tok + w], start=True, stop=True)
                        ins.then_inc(sc_full[k], 1)
                        if k == 1 and s >= LAG:
                            pv(s - LAG)
                        if more:
                            max_heads(g + 1, 1 - u, s, (2 * k, 2 * k + 1))
                    if s == 0:
                        turn_rows(CB * g + 1)
                    if s == UA + 1 and more:
                        turn_rows(CB * g + 2)
                for s in range(NS - LAG, NS):
                    pv(s)

            pe.wait_ge(m_ld[0], 16 * 2 * LOADS)
            for nu in range(NU):
                max_heads(0, 0, nu, range(HG))
                if nu == UA + 1:
                    turn_rows(0)
            pe.wait_ge(ones_ready, 7)
            with pe.Fori(0, NG // 2 - 1) as i:
                slot(i, 0, True)
                slot(i, 1, True)
            slot(NG // 2 - 1, 0, True)
            slot(NG // 2 - 1, 1, False)

            pe.wait_ge(late_ld, 32)
            pe.wait_ge(y_ready[1], PRIME + NG)
            with pe.Fori(0, NC) as n:
                pe.wait_ge(c_ld, 16 * n + 16)
                for tt in range(TT):
                    pe.wait_ge(yn_ready[tt % 2], PRIME + 2 * n + tt // 2)
                    for gg in range(GB):
                        ins = pe.transpose(YT[tt % 2][:, gg * P:(gg + 1) * P], yraw[:, gg, tt * P:(tt + 1) * P],
                                           ident[:, :])
                    ins.then_inc(yt_full, 1)
                pe.wait_ge(lo_ready, PRIME + KD * n)
                for tt in range(TT):
                    pe.wait_ge(yn_ready[tt % 2], PRIME + 2 * n + tt // 2 + 1)
                    for k in range(KD):
                        ins = pe.transpose(BIGT[:, k, tt * P:(tt + 1) * P], yn[:, tt, k * P:(k + 1) * P], ident[:, :])
                ins.then_inc(big_full, 1)
                pe.wait_ge(ynT_ready, KD * n + KD)
                for tt in range(TT):
                    pe.wait_ge(x2_ready[tt % 2], PRIME + 2 * n + tt // 2)
                    for k in range(KD):
                        ins = pe.matmul(FC[tt % 2][:, 0:D], ynT[:, k, tt * P:(tt + 1) * P], wpr[:, k, :],
                                        start=(k == 0), stop=(k == KD - 1))
                    ins.then_inc(pj_full, 1)
                for tt in range(TT):
                    pe.wait_ge(xn3, PRIME + TT * n + tt + 1)
                    for k in range(KD):
                        ins = pe.transpose(BIGT[:, k, tt * P:(tt + 1) * P], xn[:, tt, k * P:(k + 1) * P], ident[:, :])
                ins.then_inc(big_full, 1)
                pe.wait_ge(hi_ready, KD * n + KD)
                pe.wait_ge(lo_ready, PRIME + KD * n + KD)
                for j in range(HJ):
                    if j >= 2:
                        pe.wait_ge(gel_ready, HJ * n + j - 1)
                    for k in range(KD):
                        for part in (hi, lo):
                            ins = pe.matmul(FC[j % 2], fcT[:, k, j, :], part[:, k, :],
                                            start=(k == 0 and part is hi), stop=(k == KD - 1 and part is lo))
                    ins.then_inc(fc_full, 1)
                pe.wait_ge(gel_ready, HJ * n + HJ)
                for pair in range(TT // 2):
                    for fb in range(2):
                        tt = 2 * pair + fb
                        pe.wait_ge(o_ready[fb], PRIME + 2 * n + pair)
                        for j in range(HJ):
                            pe.matmul(FO[fb][:, 0:D + 1], gel[j][:, tt * P:(tt + 1) * P], w2[:, j, 0:D + 1],
                                      start=(j == 0), stop=(j == HJ - 1), skip_group_check=True)
                    pe.wait_ge(ssq_ready, PRIME + n + 1)
                    pe.wait_ge(dve_c, (8 * TT + 1) * n + 3 * TT + 1)
                    for fb in range(2):
                        tt = 2 * pair + fb
                        pe.matmul(FO[fb][:, D + 1:D + 2], ssq[:, tt * P:(tt + 1) * P], ones[:, 0:1],
                                  start=False, stop=False, skip_group_check=True)
                        pe.matmul(FO[fb][:, D + 1:D + 2], ssq2[:, tt * P:(tt + 1) * P], ones[:, 0:1],
                                  start=False, stop=True, skip_group_check=True).then_inc(fo_full[fb], 1)


_INS = ["x", "ctx_1024", "L0_xattn_W_attn", "L0_xattn_b_attn", "L0_xattn_W_proj", "L0_xattn_b_proj",
        "L0_ffn_W_fc", "L0_ffn_ln_w", "L0_ffn_ln_b", "L0_ffn_W_proj"]


def kernel(**inputs):
    import numpy as _np
    import concourse.bacc as _bacc
    from concourse import mybir as _mybir
    from concourse.bass_utils import run_bass_kernel_spmd as _run

    nc = _bacc.Bacc("TRN2", target_bir_lowering=False, num_devices=1)
    arrays, args = {}, []
    for name in _INS:
        a = _np.ascontiguousarray(inputs[name])
        arrays[f"in_{name}"] = a
        args.append(nc.dram_tensor(f"in_{name}", a.shape, _mybir.dt.from_np(a.dtype), kind="ExternalInput").ap())
    args.append(nc.dram_tensor("out_0", (B, T, D), F32, kind="ExternalOutput").ap())
    build(nc, *args)
    r = _run(nc, [arrays], core_ids=[0])
    return r.results[0]["out_0"]
```

```python
from contextlib import ExitStack

import concourse.bass as bass
from concourse import mybir

F32 = mybir.dt.float32
BF16 = mybir.dt.bfloat16
F16 = mybir.dt.float16
ALU = mybir.AluOpType
ACT = mybir.ActivationFunctionType
AX = mybir.AxisListType

B, T, D = 2, 1024, 256
MEM = 77
NH, HD = 16, 16
H = 1024
P = 128
KD = D // P
HG = 4
GB = NH // HG
NG = B * GB
S = MEM + T
KB = -(-S // P)
LAST = S - (KB - 1) * P
SP = 1104
CH = 512
NC = B * T // CH
CB = T // CH
TT = CH // P
HJ = H // P
LN_EPS = 1e-5
TERN_EPS = 1e-6
BIG = -1e30
LOWEST = -3.0e38
PAIRS = [(0, 0), (0, 1), (0, 2), (1, 0), (1, 1), (2, 0)]
KR = len(PAIRS) * HD
KM = KR + 3

BLOCKS = [[0, 3, 1, 2, 4], [0, 7, 1, 6, 2, 5, 3, 4, 8]]
STEPS = []
for _c in range(CB):
    for _j in BLOCKS[_c]:
        _lo = max(_c * CH, _j * P - MEM)
        STEPS.append((_c, _j, _lo - _c * CH, _lo, (_c + 1) * CH - _lo))
    assert sorted(BLOCKS[_c]) == [j for j in range(KB) if j * P - MEM < (_c + 1) * CH]
NS = len(STEPS)
CEND = [max(s for s, st in enumerate(STEPS) if st[0] == c) for c in range(CB)]
DIAG = []
for _c, _j, _col, _tok, _w in STEPS:
    _a, _b = max(_tok, _j * P - MEM), min(_tok + _w, _j * P - MEM + P)
    DIAG.append((_a - _tok, _b - _a) if _b > _a else None)
NDIAG = sum(d is not None for d in DIAG)
UNITS = []
for _c in range(CB):
    _u = []
    for _i in range(_c * TT, (_c + 1) * TT):
        _n = MEM + P * (_i + 1)
        _u += [(_i, _s, _s * CH, min(CH, _n - _s * CH)) for _s in range(-(-_n // CH))]
    _u.sort(key=lambda u: -u[3])
    _steps = sorted((n for n, st in enumerate(STEPS) if st[0] == _c), key=lambda n: (-STEPS[n][4], n))
    _mine = dict(zip(_steps, _u))
    UNITS += [_mine[n] for n in sorted(_mine)]
NU = len(UNITS)
assert NU == NS
UA = sum(u[0] < TT for u in UNITS)
MSLOTS = max(u[1] for u in UNITS) + 1
LOADS = len(PAIRS)
MXB = 3
ROWS_AT = (0, UA + 1)
ITEMS = HG * NU + 2


def item(nu, h):
    return HG * nu + h + sum(nu > at for at in ROWS_AT)


def rows_item(which):
    return HG * (ROWS_AT[which] + 1) + which


PRIME, DMA_PRIME = 1, 16
PB = 4
LAG = 2


def build(nc, x, ctx_in, w_attn, b_attn, w_proj, b_proj, w_fc, ln_w, ln_b, w_out, out):
    q_scr = nc.dram_tensor("q_scr", [NG, HG, HD, 3, T], BF16).ap()
    k_scr = nc.dram_tensor("k_scr", [NG, HG, HD, 3, SP], BF16).ap()
    v_scr = nc.dram_tensor("v_scr", [NG, KB * P, 2 * HG * HD], F32).ap()
    y_scr = nc.dram_tensor("y_scr", [B, GB, P, T], F32).ap()
    m_scr = nc.dram_tensor("m_scr", [3, HG * TT, P], BF16).ap()
    q_st = q_scr.rearrange("(m g) h d a t -> m (g h d) a t", g=2)
    k_st = k_scr.rearrange("(m g) h d a t -> m (g h d) a t", g=2)
    v_st_view = v_scr.rearrange("(b g) s d -> b s g d", g=GB)
    x_ch = x.rearrange("b (c i p) d -> (b c) p i d", i=TT, p=P)
    out_ch = out.rearrange("b (c i p) d -> (b c) p i d", i=TT, p=P)

    with ExitStack() as es:
        def sb(name, shape, dt=F32):
            return es.enter_context(nc.sbuf_tensor(name, shape, dt))

        def sem(name):
            return es.enter_context(nc.semaphore(name))

        def sems(name, n):
            return [sem(f"{name}{i}") for i in range(n)]

        ps = es.enter_context(nc.psum_tensor("ps", [P, 8, CH], F32))

        ident = sb("ident", [P, P])
        identh = sb("identh", [P, P], BF16)
        identt = sb("identt", [P, P], F16)
        ones = sb("ones", [P, P])
        mean_w = sb("mean_w", [P, P])
        nhalf = sb("nhalf", [P, TT])
        wqkv = sb("wqkv", [P, KD, 3 * D])
        wpr = sb("wpr", [P, KD, D])
        bqk = sb("bqk", [P, 2 * KD])
        bv = sb("bv", [P, D])
        bpr = sb("bpr", [P, D])
        lnw = sb("lnw", [P, HJ])
        lnb = sb("lnb", [P, HJ])
        fcT = sb("fcT", [P, KD, HJ, P], F16)
        w2 = sb("w2", [P, HJ, D + 2])
        c1 = sb("c1", [P, D])
        c2 = sb("c2", [P, D])
        gam = sb("gam", [P, 8])
        stq_m = [sb(f"stq_m{i}", [P, HG, T], BF16) for i in range(2)]
        stk_m = [sb(f"stk_m{i}", [P, HG, SP], BF16) for i in range(2)]
        stq_e = [sb(f"stq_e{i}", [P, HG, T], BF16) for i in range(2)]
        stk_e = [sb(f"stk_e{i}", [P, HG, SP], BF16) for i in range(2)]
        vst = [sb(f"vst{i}", [P, KB, HG, 2 * HD]) for i in range(2)]
        probs = [sb(f"probs{i}", [P, HG, CH]) for i in range(PB)]
        window = sb("window", [P, S], BF16)
        junk = [sb(f"junk{i}", [P, CH], BF16) for i in range(MXB)]
        mpart = [sb(f"mpart{i}", [P, HG, TT, MSLOTS]) for i in range(CB)]
        negm = sb("negm", [P, HG * TT])
        mres = sb("mres", [P, HG * TT])
        mparts = sb("mparts", [P, 3, HG * TT], BF16)
        mrows = sb("mrows", [3 * HG * TT, P], BF16)
        ystage = [sb(f"ystage{i}", [P, CH]) for i in range(CB)]
        raw_fc = stk_m[0][:, :, :].rearrange("p h s -> p (h s)")[:, 0:2 * HJ * D].bitcast(F32)
        raw_fc = raw_fc.rearrange("p (j d) -> p j d", d=D)
        raw_out = stk_m[1][:, :, :].rearrange("p h s -> p (h s)")[:, 0:2 * KD * H].bitcast(F32)
        raw_out = raw_out.rearrange("p (k h) -> p k h", h=H)
        tern_a = probs[0][:, :, :].rearrange("p h t -> p (h t)").bitcast(F16)[:, 0:HJ * D]
        tern_b = probs[1][:, :, :].rearrange("p h t -> p (h t)").bitcast(F16)
        tern_fcv = tern_b[:, 0:HJ * D].rearrange("p (j d) -> p j d", d=D)
        tern_outv = tern_b[:, HJ * D:2 * HJ * D].rearrange("p (k h) -> p k h", h=H)
        wT = probs[0][:, :, :].rearrange("p h t -> p (h t)")[:, 0:HJ * D].rearrange("p (j d) -> p j d", d=D)
        lnb_wide = probs[1][:, :, :].rearrange("p h t -> p (h t)")[:, 0:HJ * P].rearrange("p (j m) -> p j m", m=P)
        x_a = sb("x_a", [P, TT, D])
        xn = sb("xn", [P, TT, D])
        xnT = sb("xnT", [P, KD, CH])
        stats = sb("stats", [P, TT, 6])
        mv = sb("mv", [P, TT, 2])
        ve = sb("ve", [P, TT])
        rs = sb("rs", [P, TT])
        late_parts = probs[2][:, :, :].rearrange("p h t -> p (h t)").bitcast(BF16)
        parts = [sb(f"parts{i}", [P, 3, CH], BF16) for i in range(2)]
        parts += [late_parts[:, i * 3 * CH:(i + 1) * 3 * CH].rearrange("p (a t) -> p a t", t=CH) for i in range(2)]
        resid = [sb(f"resid{i}", [P, CH]) for i in range(2)] + [probs[3][:, i, :] for i in range(2)]
        vtile = sb("vtile", [P, TT, NH, 2 * HD])
        vctx = sb("vctx", [MEM, B, NH, 2 * HD])
        ctx_t = sb("ctx_t", [MEM, B, D])
        ctx_p = sb("ctx_p", [P, 3, B * KD, MEM], BF16)
        ctx_r = sb("ctx_r", [P, B * KD * MEM])
        rden = [sb(f"rden{i}", [P, 2 * NH]) for i in range(2)]

        def room(t, first, shape, dt=F32):
            v = t[:, :, :].rearrange("p a b -> p (a b)").bitcast(F32)
            a, b = shape
            words = a * b // (1 if dt == F32 else 2)
            v = v[:, first:first + words]
            return (v if dt == F32 else v.bitcast(dt)).rearrange("p (a b) -> p a b", b=b)

        yraw = room(stq_m[0], 0, (GB, CH))
        yn = room(stq_m[1], 0, (TT, D))
        ynT = room(stq_m[1], TT * D, (KD, CH))
        xb = room(stk_m[0], 0, (TT, D))
        x2 = room(stk_m[0], TT * D, (TT, D))
        x2c = room(stk_m[1], 0, (TT, D))
        o_t = room(stk_m[1], TT * D, (TT, D))
        hi = room(stq_e[1], 0, (KD, CH), F16)
        lo = room(stq_e[1], KD * CH // 2, (KD, CH), F16)
        g_lo = stk_e[0][:, :, :].rearrange("p h s -> p (h s)")[:, 0:HJ * CH].bitcast(F32)
        g_hi = stq_e[0][:, :, :].rearrange("p h s -> p (h s)")[:, 0:HJ * CH].bitcast(F32)
        gel = [(g_lo if j < HJ // 2 else g_hi)[:, (j % (HJ // 2)) * CH:(j % (HJ // 2) + 1) * CH] for j in range(HJ)]
        sq = probs
        ssq2 = sb("ssq2", [P, CH])
        ssq = sb("ssq", [P, CH])
        moments = [sb(f"moments{i}", [P, 2, 2]) for i in range(2)]
        msq = [sb(f"msq{i}", [P, 2]) for i in range(2)]
        ve_h = [sb(f"ve_h{i}", [P, 2]) for i in range(2)]
        rs_h = [sb(f"rs_h{i}", [P, 2]) for i in range(2)]
        t1 = sb("t1", [P, 2, D])

        fc_ld, wo_ld, small_ld, qkvw_ld = sem("fc_ld"), sem("wo_ld"), sem("small_ld"), sem("qkvw_ld")
        late_ld, ctx_ld = sem("late_ld"), sem("ctx_ld")
        dve_w, dve_a, dve_b, pool_own = sem("dve_w"), sem("dve_a"), sem("dve_b"), sem("pool_own")
        const_ready, ones_ready = sem("const_ready"), sem("ones_ready")
        abs_ready, gam_full = sem("abs_ready"), sem("gam_full")
        tern_ready, wt_full, wt_read = sem("tern_ready"), sem("wt_full"), sem("wt_read")
        w2_ready, cc_full, cc_read = sem("w2_ready"), sem("cc_full"), sem("cc_read")
        ctx_full, ctx_p1, ctx_p2, ctx_p3 = sem("ctx_full"), sem("ctx_p1"), sem("ctx_p2"), sem("ctx_p3")
        ctx_st, vctx_ready = sem("ctx_st"), sem("vctx_ready")
        x_ld = sem("x_ld")
        ve_ready, rs_ready, xn_ready = sem("ve_ready"), sem("rs_ready"), sem("xn_ready")
        xT_full, xT_evac = sem("xT_full"), sem("xT_evac")
        qk_full, p1_ready, p2_ready, p3_ready = sem("qk_full"), sem("p1_ready"), sem("p2_ready"), sem("p3_ready")
        r_ready, v_full, v_ready = sem("r_ready"), sem("v_full"), sem("v_ready")
        qk_st, v_st = sems("qk_st", 2 * KD), sems("v_st", TT)
        m_ld = sems("m_ld", 2)
        e_ld = sems("e_ld", 2)
        vs_ld = sems("vs_ld", 2)
        mx_full, mx_read, mp_ready = sem("mx_full"), sem("mx_read"), sem("mp_ready")
        mr_st, mr_ld = sem("mr_st"), sem("mr_ld")
        sc_full, pr_ready, sel_ready = sems("sc_full", 2), sems("pr_ready", 2), sems("sel_ready", 2)
        pv_done = sem("pv_done")
        y_ready, y_st = sems("y_ready", CB), sems("y_st", CB)
        c_ld, x3_ld, xb_ready = sem("c_ld"), sem("x3_ld"), sem("xb_ready")
        yt_full, yn_ready, dve_y = sem("yt_full"), sem("yn_ready"), sem("dve_y")
        at_full, ynT_ready = sem("at_full"), sem("ynT_ready")
        pj_full, x2_ready, dve_x, x2c_ready = sem("pj_full"), sem("x2_ready"), sem("dve_x"), sem("x2c_ready")
        ve3, rs3, xn3, ln_full = sem("ve3"), sem("rs3"), sem("xn3"), sem("ln_full")
        hi_ready, lo_ready = sem("hi_ready"), sem("lo_ready")
        fc_full, gel_ready, sq_ready, ssq_ready = sem("fc_full"), sem("gel_ready"), sems("sq_ready", 2), sem("ssq_ready")
        fo_full, fo_read, dve_e, ve4, rs4 = sem("fo_full"), sem("fo_read"), sem("dve_e"), sem("ve4"), sem("rs4")
        o_ready, o_st = sem("o_ready"), sem("o_st")

        XT = ps[:, 0:2, :]
        QK = [ps[:, 2, :], ps[:, 3, :], ps[:, 6, :], ps[:, 7, :]]
        VV = [ps[:, 4, 0:D], ps[:, 5, 0:D]]
        CT = ps[:, 6, 0:B * KD * MEM]
        WT = [ps[:, 6, :].bitcast(F16), ps[:, 7, :].bitcast(F16)]
        CC = [ps[:, 0, 0:D], ps[:, 1, 0:D]]
        SC = [ps[:, 0:2, :], ps[:, 2:4, :]]
        MX = [ps[:, b, :] for b in (4, 5, 7)]
        ACC = ps[:, 6, :]
        MT = [mx[0:3 * HG * TT, 0:P // 2].bitcast(BF16) for mx in MX]
        YT = [ps[:, 0:2, :], ps[:, 2:4, :]]
        AT, LN = ps[:, 0:2, :], ps[:, 2:4, :]
        FC = [ps[:, 4, :], ps[:, 5, :]]
        FO = ps[:, 6:8, :]

        block = es.enter_context(nc.Block())

        def not_first(n):
            return not isinstance(n, int) or n > 0

        def prime(eng, value, *signals):
            for signal in signals:
                eng.sem_inc(signal, value)

        def wait_apart(eng, *waits):
            waits = [(signal, count if isinstance(count, int) else eng.to_reg(count)) for signal, count in waits]
            eng.wait_ge(const_ready, 6)
            for signal, count in waits:
                eng.wait_ge(signal, count)

        def items_before(g, local):
            if isinstance(g, int) and g == -1 and local <= rows_item(0):
                return local
            if isinstance(g, int) and g == NG - 1:
                local -= HG * (ROWS_AT[0] + 1)
            return ITEMS * (g + 1) + local - 1

        def bank_free(g, local):
            earlier = local - MXB
            if earlier >= 0:
                return items_before(g, earlier) + 1
            if isinstance(g, int) and g == -1:
                return 0
            return items_before(g - 1, max(k for k in range(ITEMS) if k % MXB == local % MXB)) + 1

        def wait_all(eng, *waits):
            waits = [(sig, count if isinstance(count, int) else eng.to_reg(count)) for sig, count in waits]
            for signal, count in waits:
                eng.wait_ge(signal, count)

        def occ(i, off):
            return i + off // 2

        @block.sync
        def _(sp):
            prime(sp, PRIME, *sc_full)
            def load_x(n):
                if not_first(n):
                    sp.wait_ge(xn_ready, TT * n)
                sp.dma_start(x_a[:, :, :], x_ch[n]).then_inc(x_ld, 16)

            for b in range(B):
                sp.dma_start(ctx_t[:, b, :], ctx_in[b]).then_inc(ctx_ld, 16)
            load_x(0)
            sp.dma_start(wqkv[:, :, :], w_attn.rearrange("(k p) n -> p k n", p=P)).then_inc(qkvw_ld, 16)
            sp.dma_start(bqk[:, :], b_attn[0:2 * D].rearrange("(m p) -> p m", p=P),
                         allow_slow_non_contiguous=True).then_inc(qkvw_ld, 16)
            sp.dma_start(bv[:, :], b_attn[2 * D:3 * D].partition_broadcast(P)).then_inc(qkvw_ld, 16)
            sp.dma_start(raw_fc, w_fc.rearrange("(p j) d -> p j d", j=HJ)).then_inc(fc_ld, 16)
            sp.dma_start(raw_out, w_out.rearrange("(k p) h -> p k h", p=P)).then_inc(wo_ld, 16)
            load_x(1)
            sp.dma_start(lnw[:, :], ln_w.rearrange("(p j) -> p j", j=HJ)).then_inc(small_ld, 16)
            sp.dma_start(lnb[:, :], ln_b.rearrange("(p j) -> p j", j=HJ)).then_inc(small_ld, 16)
            sp.dma_start(wpr[:, :, :], w_proj.rearrange("(k p) n -> p k n", p=P)).then_inc(late_ld, 16)
            sp.dma_start(bpr[:, :], b_proj.partition_broadcast(P)).then_inc(late_ld, 16)
            sp.wait_ge(vctx_ready, 2)
            for b in range(B):
                sp.dma_start(v_st_view[b, 0:MEM], vctx[:, b, :, :].rearrange("p (g h) d -> p g (h d)", g=GB))\
                    .then_inc(ctx_st, 16)
            for a, part_ready in enumerate((ctx_p1, ctx_p2, ctx_p3)):
                sp.wait_ge(part_ready, 1)
                sp.dma_start(k_st[:, :, a, 0:MEM].rearrange("m r t -> r m t"), ctx_p[:, a, :, :]).then_inc(ctx_st, 16)

            q_tiles = q_st.rearrange("(b k) r a (c t) -> b c k r a t", k=KD, c=CB)
            k_tiles = k_st[:, :, :, MEM:S].rearrange("(b k) r a (c t) -> b c k r a t", k=KD, c=CB)
            v_tiles = v_st_view[:, MEM:S].rearrange("b (c i p) g d -> b c i p g d", i=TT, p=P)

            def store_chunk(n, more):
                for m in range(2 * KD):
                    sp.wait_ge(p3_ready, 2 * KD * n + m + 1)
                    dst = (q_tiles if m < KD else k_tiles)[n // CB, n % CB, m % KD]
                    sp.dma_start(dst, parts[m][:, :, :]).then_inc(qk_st[m], 16)
                    if m == 1 and more:
                        load_x(n + 2)
                for tt in range(TT):
                    sp.wait_ge(v_ready, TT * n + tt + 1)
                    sp.dma_start(v_tiles[n // CB, n % CB, tt],
                                 vtile[:, tt, :, :].rearrange("p (g h) d -> p g (h d)", g=GB)).then_inc(v_st[tt], 16)

            def stored(chunks):
                for done in qk_st + v_st:
                    sp.wait_ge(done, 16 * chunks)

            def load_stack(q_dst, k_dst, g, done):
                for r, (qa, ka) in enumerate(PAIRS):
                    rows = slice(r * HD, (r + 1) * HD)
                    sp.dma_start(q_dst[rows, :, :], q_scr[g, :, :, qa, :].rearrange("h d t -> d h t")).then_inc(done, 16)
                    sp.dma_start(k_dst[rows, :, 0:S], k_scr[g, :, :, ka, 0:S].rearrange("h d t -> d h t"))\
                        .then_inc(done, 16)

            def load_values(v_dst, g, done):
                sp.dma_start(v_dst[:, 0:KB - 1, :, :].rearrange("p j h d -> p j (h d)"),
                             v_scr[g, 0:(KB - 1) * P, :].rearrange("(j p) d -> p j d", p=P)).then_inc(done, 16)
                sp.dma_start(v_dst[0:LAST, KB - 1, :, :].rearrange("p h d -> p (h d)"),
                             v_scr[g, (KB - 1) * P:S, :]).then_inc(done, 16)

            def copy_stack(par, loads, *before):
                wait_all(sp, *before, (m_ld[par], 16 * 2 * LOADS * loads))
                sp.dma_start(stq_e[par][0:KR, :, :], stq_m[par][0:KR, :, :]).then_inc(e_ld[par], 16)
                sp.dma_start(stk_e[par][0:KR, :, 0:S], stk_m[par][0:KR, :, 0:S]).then_inc(e_ld[par], 16)

            def place_max_rows(par, c, q, g):
                sp.wait_ge(mx_read, items_before(g, rows_item(1 - c)) + 1)
                sp.dma_start(m_scr.rearrange("a r t -> (a r) t"), mrows[:, :]).then_inc(mr_st, 16)
                sp.wait_ge(mr_st, 16 * q + 16)
                sp.dma_start(stq_e[par][KR:KM, :, c * CH:(c + 1) * CH],
                             m_scr.rearrange("a (h i) t -> a h (i t)", h=HG)).then_inc(mr_ld, 16)

            with sp.Fori(0, NC - 2) as n:
                store_chunk(n, True)
            assert CB == 2 and NC == B * CB
            stored(CB)
            sp.wait_ge(ctx_st, 16 * (B + 3))
            sp.wait_ge(tern_ready, 2)
            load_stack(stq_m[0], stk_m[0], 0, m_ld[0])
            with sp.Fori(NC - 2, NC) as n:
                store_chunk(n, False)
            load_stack(stq_m[1], stk_m[1], 1, m_ld[1])
            load_values(vst[0], 0, vs_ld[0])
            copy_stack(0, 1)
            stored(NC)
            place_max_rows(0, 0, 0, -1)

            def slot(i, u, more_m, more_e):
                g = 2 * i + u
                place_max_rows(u, 1, 2 * g + 1, g)
                if more_e:
                    copy_stack(1 - u, occ(i, u + 1) + 1, (sc_full[1], PRIME + NS * g))
                if more_m:
                    wait_all(sp, (mx_full, items_before(g, 0)), (e_ld[u], 16 * 2 * (i + 1)))
                    load_stack(stq_m[u], stk_m[u], g + 2, m_ld[u])
                if more_e:
                    sp.wait_ge(pv_done, PB + NS * g)
                    load_values(vst[1 - u], g + 1, vs_ld[1 - u])
                sp.wait_ge(y_ready[0], PRIME + g + 1)
                sp.dma_start(y_scr[g // GB, g % GB, :, 0:CH], ystage[0][:, :]).then_inc(y_st[0], 16)
                if more_e:
                    place_max_rows(1 - u, 0, 2 * g + 2, g)
                sp.wait_ge(y_ready[1], PRIME + g + 1)
                sp.dma_start(y_scr[g // GB, g % GB, :, CH:T], ystage[1][:, :]).then_inc(y_st[1], 16)

            with sp.Fori(0, NG // 2 - 1) as i:
                slot(i, 0, True, True)
                slot(i, 1, True, True)
            slot(NG // 2 - 1, 0, False, True)
            slot(NG // 2 - 1, 1, False, False)

            for c in range(CB):
                sp.wait_ge(y_st[c], DMA_PRIME + 16 * NG)
            y_ch = y_scr.rearrange("b g p (c t) -> b c p g t", c=CB)

            def load(n):
                if not_first(n):
                    sp.wait_ge(yt_full, 2 * n)
                sp.dma_start(yraw[:, :, :], y_ch[n // CB, n % CB]).then_inc(c_ld, 16)
                if not_first(n):
                    sp.wait_ge(xb_ready, n)
                sp.dma_start(x_a[:, :, :], x_ch[n]).then_inc(x3_ld, 16)

            def store(n):
                sp.wait_ge(o_ready, TT * n + TT)
                sp.dma_start(out_ch[n], o_t[:, :, :]).then_inc(o_st, 16)

            load(0)
            load(1)
            with sp.Fori(2, NC) as n:
                load(n)
                store(n - 2)
            store(NC - 2)
            store(NC - 1)
            sp.wait_ge(o_st, DMA_PRIME + 16 * NC)

        @block.gpsimd
        def _(pool):
            for t in (ident, identh, identt):
                pool.memset(t[:, :], 0.0).then_inc(pool_own, 1)
            pool.memset(window[:, :], 0.0).then_inc(pool_own, 1)
            pool.wait_ge(pool_own, 4)
            for t in (ident, identh, identt):
                pool.affine_select(out=t[:, :], in_=t[:, :], compare_op=ALU.not_equal, fill=1.0, base=0,
                                   pattern=[[-1, P]], channel_multiplier=1).then_inc(const_ready, 1)
            pool.affine_select(out=window[:, S - P:S], in_=window[:, S - P:S], compare_op=ALU.is_ge, fill=BIG,
                               base=0, pattern=[[-1, P]], channel_multiplier=1).then_inc(const_ready, 1)
            pool.memset(ones[:, :], 1.0).then_inc(const_ready, 1)
            pool.memset(nhalf[:, :], -0.5).then_inc(pool_own, 1)
            pool.memset(mean_w[:, :], 1.0 / (H * D)).then_inc(const_ready, 1)
            pool.memset(vtile[:, :, :, HD:2 * HD].rearrange("p i h d -> p (i h) d"), 1.0).then_inc(ones_ready, 1)
            pool.memset(vctx[:, :, :, HD:2 * HD], 1.0).then_inc(vctx_ready, 1)
            for c in range(CB):
                pool.memset(mpart[c][:, :, :, :], LOWEST).then_inc(ones_ready, 1)
            pool.memset(w2[:, :, D:D + 2], 1.0 / H).then_inc(ones_ready, 1)
            pool.wait_ge(pool_own, 5)
            pool.wait_ge(ctx_p2, 1)
            pool.tensor_tensor(ctx_p[:, 2, :, :].rearrange("p m t -> p (m t)"), ctx_r[:, :],
                               ctx_p[:, 1, :, :].rearrange("p m t -> p (m t)"), ALU.subtract).then_inc(ctx_p3, 1)
            def token_deviations(n):
                pool.wait_ge(ve_ready, n + 1)
                pool.tensor_tensor(rs[:, :], ve[:, :], nhalf[:, :], ALU.pow).then_inc(rs_ready, 1)

            def third_parts(n):
                for m in range(2 * KD):
                    pool.wait_ge(p2_ready, 2 * KD * n + m + 1)
                    pool.tensor_tensor(parts[m][:, 2, :], resid[m][:, :], parts[m][:, 1, :],
                                       ALU.subtract).then_inc(p3_ready, 1)

            token_deviations(0)
            with pool.Fori(0, NC - 1) as n:
                token_deviations(n + 1)
                third_parts(n)
            third_parts(NC - 1)
            pool.wait_ge(small_ld, 32)
            pool.wait_ge(wt_read, 2 * KD)
            pool.tensor_tensor(w2[:, :, 0:D], wT, lnw[:, :].rearrange("p (j o) -> p j o", o=1).to_broadcast([P, HJ, D]),
                               ALU.mult).then_inc(w2_ready, 1)
            pool.tensor_copy(lnb_wide, lnb[:, :].rearrange("p (j o) -> p j o", o=1).to_broadcast([P, HJ, P]))\
                .then_inc(w2_ready, 1)

            def slot(i, u):
                g = 2 * i + u
                for s, (c, j, col, tok, w) in enumerate(STEPS):
                    if DIAG[s] is None:
                        continue
                    a, dw = DIAG[s]
                    rows = P if j < KB - 1 else LAST
                    for k in range(2):
                        wait_apart(pool, (pr_ready[k], PRIME + NS * g + s + 1))
                        part = probs[(NS * u + s) % PB][0:rows, 2 * k:2 * k + 2, a:a + dw]
                        pool.affine_select(out=part, in_=part, compare_op=ALU.is_ge, fill=0.0,
                                           base=tok + a + MEM - P * j, pattern=[[0, 2], [1, dw]],
                                           channel_multiplier=-1).then_inc(sel_ready[k], 1)

            with pool.Fori(0, NG // 2) as i:
                slot(i, 0)
                slot(i, 1)

            pool.wait_ge(late_ld, 32)
            pool.wait_ge(cc_read, 2)

            def with_bias(n):
                pool.wait_ge(x3_ld, 16 * n + 16)
                if not_first(n):
                    pool.wait_ge(x2_ready, 2 * n)
                pool.tensor_tensor(xb[:, :, :], x_a[:, :, :],
                                   bpr[:, :].rearrange("p (o d) -> p o d", o=1).to_broadcast([P, TT, D]),
                                   ALU.add).then_inc(xb_ready, 1)

            def deviations(n):
                pool.wait_ge(ve3, n + 1)
                pool.tensor_tensor(rs[:, :], ve[:, :], nhalf[:, :], ALU.pow).then_inc(rs3, 1)

            def hidden_deviations(n, pair):
                pool.wait_ge(ve4, 2 * n + pair + 1)
                pool.tensor_tensor(rs_h[pair][:, :], ve_h[pair][:, :], nhalf[:, 0:2], ALU.pow).then_inc(rs4, 1)

            def squares(n):
                for j in range(HG):
                    pool.wait_ge(gel_ready, HJ * n + j + 1)
                    pool.tensor_tensor(sq[0][:, j, :], gel[j], gel[j], ALU.mult).then_inc(sq_ready[0], 1)

            def with_c2(n):
                if not_first(n):
                    pool.wait_ge(o_ready, TT * n)
                pool.tensor_tensor(x2c[:, :, :], x2[:, :, :],
                                   c2[:, :].rearrange("p (o d) -> p o d", o=1).to_broadcast([P, TT, D]),
                                   ALU.add).then_inc(x2c_ready, 1)

            with_bias(0)
            deviations(0)
            squares(0)
            with_c2(0)
            with pool.Fori(1, NC) as n:
                with_bias(n)
                hidden_deviations(n - 1, 0)
                deviations(n)
                hidden_deviations(n - 1, 1)
                squares(n)
                with_c2(n)
            hidden_deviations(NC - 1, 0)
            hidden_deviations(NC - 1, 1)

        @block.scalar
        def _(act):
            prime(act, PB, pv_done)
            prime(act, DMA_PRIME, *y_st)
            act.wait_ge(ctx_full, 1)
            act.activation(ctx_p[:, 0, :, :].rearrange("p m t -> p (m t)"), CT, ACT.Copy).then_inc(ctx_p1, 1)

            def turned_chunk(n):
                act.wait_ge(xT_full, n + 1)
                if not_first(n):
                    act.wait_ge(v_full, TT * n)
                for k in range(KD):
                    act.activation(xnT[:, k, :], XT[:, k, :], ACT.Copy).then_inc(xT_evac, 1)

            def first_parts(n):
                for m in range(2 * KD):
                    act.wait_ge(qk_full, 2 * KD * n + m + 1)
                    if not_first(n):
                        act.wait_ge(qk_st[m], 16 * n)
                    act.activation(parts[m][:, 0, :], QK[m], ACT.Identity, bias=bqk[:, m:m + 1]).then_inc(p1_ready, 1)

            turned_chunk(0)
            act.wait_ge(qkvw_ld, 48)
            first_parts(0)
            for r in range(2 * KD):
                act.wait_ge(wt_full, r + 1)
                k = r % KD
                src = WT[r % 2].rearrange("p (j c) -> p j c", c=P)
                dst = fcT[:, k, :, :] if r < KD else wT[:, :, k * P:(k + 1) * P]
                act.activation(dst, src, ACT.Copy).then_inc(wt_read, 1)
            turned_chunk(1)
            with act.Fori(1, NC - 1) as n:
                first_parts(n)
                turned_chunk(n + 1)
            first_parts(NC - 1)
            for which, dst in enumerate((c1, c2)):
                act.wait_ge(cc_full, which + 1)
                act.activation(dst[:, :], CC[which], ACT.Copy, scale=(-1.0, 1.0)[which]).then_inc(cc_read, 1)

            def slot(i, u):
                g = 2 * i + u

                def save(c):
                    act.wait_ge(pv_done, PB + NS * g + CEND[c] + 1)
                    act.wait_ge(y_st[c], DMA_PRIME + 16 * g)
                    act.activation(ystage[c][:, :], ACC, ACT.Copy).then_inc(y_ready[c], 1)

                for s, (c, j, col, tok, w) in enumerate(STEPS):
                    rows = P if j < KB - 1 else LAST
                    for k in range(2):
                        act.wait_ge(sc_full[k], PRIME + NS * g + s + 1)
                        act.wait_ge(pv_done, NS * g + s + 1)
                        act.activation(probs[(NS * u + s) % PB][0:rows, 2 * k:2 * k + 2, 0:w], SC[k][0:rows, :, 0:w],
                                       ACT.Exp, scale=HD ** -0.5).then_inc(pr_ready[k], 1)
                    if s == CEND[0] + LAG:
                        save(0)
                save(1)

            with act.Fori(0, NG // 2) as i:
                slot(i, 0)
                slot(i, 1)

            with act.Fori(0, NC) as n:
                act.wait_ge(at_full, n + 1)
                for k in range(KD):
                    act.activation(ynT[:, k, :], AT[:, k, :], ACT.Copy).then_inc(ynT_ready, 1)
                act.wait_ge(ln_full, n + 1)
                for k in range(KD):
                    act.activation(hi[:, k, :], LN[:, k, :], ACT.Copy).then_inc(hi_ready, 1)
                for j in range(HJ):
                    act.wait_ge(fc_full, HJ * n + j + 1)
                    act.activation(gel[j], FC[j % 2], ACT.Gelu).then_inc(gel_ready, 1)
                for j in range(HG, HJ):
                    act.wait_ge(gel_ready, HJ * n + j + 1)
                    act.activation(sq[1][:, j % HG, :], gel[j], ACT.Square).then_inc(sq_ready[1], 1)

        @block.vector
        def _(dve):
            prime(dve, DMA_PRIME, o_st)
            own = [0]

            def chain(ins, signal=dve_w):
                own[0] += 1
                ins.then_inc(signal, 1)
                dve.wait_ge(signal, own[0])

            for par in range(2):
                dve.memset(stk_e[par][KR:KM, :, :], 1.0).then_inc(ones_ready, 1)
            dve.wait_ge(ctx_ld, 16 * B)
            dve.tensor_copy(vctx[:, :, :, 0:HD], ctx_t[:, :, :].rearrange("p b (h d) -> p b h d", d=HD))\
                .then_inc(vctx_ready, 1)
            dve.wait_ge(ctx_p1, 1)
            flat = [ctx_p[:, a, :, :].rearrange("p m t -> p (m t)") for a in range(3)]
            chain(dve.tensor_tensor(ctx_r[:, :], CT, flat[0], ALU.subtract))
            dve.tensor_copy(flat[1], ctx_r[:, :]).then_inc(ctx_p2, 1)

            def token_statistics(n):
                dve.wait_ge(x_ld, 16 * n + 16)
                for tt in range(TT):
                    dve.bn_stats(stats[:, tt, :], x_a[:, tt, :]).then_inc(dve_a, 1)
                wait_apart(dve, (dve_a, 2 * TT * n + TT))
                for tt in range(TT):
                    dve.bn_aggr(mv[:, tt, :], stats[:, tt, :]).then_inc(dve_a, 1)
                dve.wait_ge(dve_a, 2 * TT * n + 2 * TT)
                dve.tensor_scalar(ve[:, :], mv[:, :, 1], LN_EPS, None, ALU.add).then_inc(ve_ready, 1)

            def normalise_tokens(n):
                dve.wait_ge(rs_ready, n + 1)
                if not_first(n):
                    dve.wait_ge(xT_full, n)
                for tt in range(TT):
                    dve.tensor_scalar(xn[:, tt, :], x_a[:, tt, :], mv[:, tt, 0:1], rs[:, tt:tt + 1],
                                      ALU.subtract, ALU.mult).then_inc(xn_ready, 1)

            def second_parts(n, tiles):
                for m in tiles:
                    dve.wait_ge(p1_ready, 2 * KD * n + m + 1)
                    if not_first(n):
                        dve.wait_ge(p3_ready, 2 * KD * (n - 1) + m + 1)
                    dve.scalar_tensor_tensor(resid[m][:, :], QK[m], bqk[:, m:m + 1], parts[m][:, 0, :],
                                             ALU.add, ALU.subtract).then_inc(r_ready, 1)
                    dve.wait_ge(r_ready, 2 * KD * n + m + 1)
                    dve.tensor_copy(parts[m][:, 1, :], resid[m][:, :]).then_inc(p2_ready, 1)

            def value_tiles(n):
                for tt in range(TT):
                    dve.wait_ge(v_full, TT * n + tt + 1)
                    if not_first(n):
                        dve.wait_ge(v_st[tt], 16 * n)
                    dve.tensor_tensor(vtile[:, tt, :, 0:HD], VV[tt % 2].rearrange("p (h d) -> p h d", d=HD),
                                      bv[:, :].rearrange("p (h d) -> p h d", d=HD), ALU.add).then_inc(v_ready, 1)

            def absolute_sums():
                dve.wait_ge(fc_ld, 16)
                dve.tensor_reduce(gam[:, 0:1], raw_fc, AX.XY, ALU.add, apply_absolute_value=True).then_inc(abs_ready, 1)
                dve.wait_ge(wo_ld, 16)
                dve.tensor_reduce(gam[:, 1:2], raw_out, AX.XY, ALU.add, apply_absolute_value=True)\
                    .then_inc(abs_ready, 1)

            def ternarise():
                dve.wait_ge(gam_full, 1)
                chain(dve.tensor_scalar(gam[:, 2:4], VV[0][:, 0:2], TERN_EPS, 0.5, ALU.add, ALU.mult))
                chain(dve.tensor_scalar(gam[:, 4:6], gam[:, 2:4], -1.0, None, ALU.mult))
                for which, (raw, dst) in enumerate(((raw_fc, tern_fcv), (raw_out, tern_outv))):
                    r2 = raw.rearrange("p a b -> p (a b)")
                    chain(dve.tensor_scalar(tern_a, r2, gam[:, 4 + which:5 + which], None, ALU.is_lt))
                    dve.scalar_tensor_tensor(dst.rearrange("p a b -> p (a b)"), r2, gam[:, 2 + which:3 + which],
                                             tern_a, ALU.is_gt, ALU.subtract).then_inc(tern_ready, 1)
                    dve.wait_ge(tern_ready, which + 1)

            token_statistics(0)
            normalise_tokens(0)
            absolute_sums()
            dve.wait_ge(qkvw_ld, 48)
            dve.wait_ge(ones_ready, 6)
            second_parts(0, (0, 1))
            token_statistics(1)
            second_parts(0, (2, 3))
            ternarise()
            normalise_tokens(1)
            value_tiles(0)
            with dve.Fori(1, NC - 1) as n:
                token_statistics(n + 1)
                second_parts(n, (0, 1))
                normalise_tokens(n + 1)
                second_parts(n, (2, 3))
                value_tiles(n)
            second_parts(NC - 1, range(2 * KD))
            value_tiles(NC - 1)

            def unit(G, nu):
                qi, slot_, key, w = UNITS[nu]
                c, ti = qi // TT, qi % TT
                start = S - (MEM + P * (qi + 1)) + key
                for h in range(HG):
                    local = item(nu, h)
                    wait_apart(dve, (mx_full, items_before(G - 1, local) + 1))
                    dve.tensor_tensor_reduce(junk[local % MXB][:, 0:w], MX[local % MXB][:, 0:w], window[:, start:start + w],
                                             1.0, LOWEST, ALU.add, ALU.max, mpart[c][:, h, ti, slot_:slot_ + 1])\
                        .then_inc(mx_read, 1)

            def split_max(G, c):
                q = CB * G + c
                dve.wait_ge(mx_read, items_before(G - 1, item((UA if c == 0 else NU) - 1, HG - 1)) + 1)
                dve.tensor_reduce(negm[:, :], mpart[c][:, :, :, :], AX.X, ALU.max, negate=True).then_inc(dve_b, 1)
                dve.wait_ge(dve_b, 4 * q + 1)
                dve.tensor_copy(mparts[:, 0, :], negm[:, :]).then_inc(dve_b, 1)
                dve.wait_ge(dve_b, 4 * q + 2)
                dve.tensor_tensor(mres[:, :], negm[:, :], mparts[:, 0, :], ALU.subtract).then_inc(dve_b, 1)
                dve.wait_ge(dve_b, 4 * q + 3)
                dve.tensor_copy(mparts[:, 1, :], mres[:, :]).then_inc(dve_b, 1)
                dve.wait_ge(dve_b, 4 * q + 4)
                dve.tensor_tensor(mparts[:, 2, :], mres[:, :], mparts[:, 1, :], ALU.subtract).then_inc(mp_ready, 1)

            def rows_out(q, which, g):
                dve.wait_ge(mx_full, items_before(g, rows_item(which)) + 1)
                if not_first(q):
                    dve.wait_ge(mr_st, 16 * q)
                dve.tensor_copy(mrows[:, :], MT[rows_item(which) % MXB]).then_inc(mx_read, 1)

            def max_pass(G, first_rows):
                for nu in range(NU):
                    unit(G, nu)
                    if nu == ROWS_AT[0] and first_rows is not None:
                        rows_out(first_rows, 0, G - 1)
                    if nu == UA - 1:
                        split_max(G, 0)
                    if nu == ROWS_AT[1]:
                        rows_out(CB * G, 1, G - 1)
                split_max(G, 1)

            dve.wait_ge(const_ready, 6)
            dve.wait_ge(ones_ready, 6)
            max_pass(0, None)
            with dve.Fori(0, NG // 2 - 1) as i:
                for u in range(2):
                    max_pass(2 * i + u + 1, CB * (2 * i + u) + 1)
            max_pass(NG - 1, CB * (NG - 2) + 1)
            rows_out(CB * (NG - 1) + 1, 0, NG - 1)


            def normalise(n):
                for pair in range(2):
                    tiles = slice(2 * pair, 2 * pair + 2)
                    dve.wait_ge(yt_full, 2 * n + pair + 1)
                    y4 = YT[pair].rearrange("p t (h r) -> p (t h) r", r=2 * HD)
                    dve.reciprocal(rden[pair][:, :], y4[:, :, HD]).then_inc(dve_y, 1)
                    dve.wait_ge(dve_y, 2 * n + pair + 1)
                    dve.tensor_tensor(yn[:, tiles, :].rearrange("p t (h d) -> p (t h) d", d=HD), y4[:, :, 0:HD],
                                      rden[pair][:, :].rearrange("p (h o) -> p h o", o=1).to_broadcast([P, 2 * NH, HD]),
                                      ALU.mult).then_inc(yn_ready, 1)

            def second_norm(n):
                dve.wait_ge(xb_ready, n + 1)
                if not_first(n):
                    dve.wait_ge(x2c_ready, n)
                for pair in range(2):
                    tiles = slice(2 * pair, 2 * pair + 2)
                    dve.wait_ge(pj_full, 2 * n + pair + 1)
                    dve.tensor_tensor(x2[:, tiles, :], FC[pair].rearrange("p (t d) -> p t d", d=D), xb[:, tiles, :],
                                      ALU.add).then_inc(x2_ready, 1)
                    dve.wait_ge(x2_ready, 2 * n + pair + 1)
                    for tt in range(2 * pair, 2 * pair + 2):
                        dve.bn_stats(stats[:, tt, :], x2[:, tt, :]).then_inc(dve_x, 1)
                wait_apart(dve, (dve_x, 2 * TT * n + TT))
                for tt in range(TT):
                    dve.bn_aggr(mv[:, tt, :], stats[:, tt, :]).then_inc(dve_x, 1)
                dve.wait_ge(dve_x, 2 * TT * n + 2 * TT)
                dve.tensor_scalar(ve[:, :], mv[:, :, 1], LN_EPS, None, ALU.add).then_inc(ve3, 1)
                dve.wait_ge(rs3, n + 1)
                for tt in range(TT):
                    dve.tensor_scalar(xn[:, tt, :], x2[:, tt, :], mv[:, tt, 0:1], rs[:, tt:tt + 1],
                                      ALU.subtract, ALU.mult).then_inc(xn3, 1)

            def low_parts(n):
                for k in range(KD):
                    dve.wait_ge(hi_ready, KD * n + k + 1)
                    dve.tensor_tensor(lo[:, k, :], LN[:, k, :], hi[:, k, :], ALU.subtract).then_inc(lo_ready, 1)

            def sum_squares(n, half):
                dve.wait_ge(sq_ready[half], HG * n + HG)
                dve.tensor_reduce((ssq, ssq2)[half][:, :], sq[half][:, :, :].rearrange("p j t -> p t j"), AX.X,
                                  ALU.add).then_inc(ssq_ready, 1)

            def finish(n, pair):
                if pair == 0:
                    dve.wait_ge(x2c_ready, n + 1)
                    dve.wait_ge(o_st, DMA_PRIME + 16 * n)
                dve.wait_ge(fo_full, 2 * n + pair + 1)
                own_base = 6 * n + 3 * pair
                dve.tensor_copy(moments[pair][:, :, :], FO[:, :, D:D + 2]).then_inc(dve_e, 1)
                dve.wait_ge(dve_e, own_base + 1)
                dve.tensor_tensor(msq[pair][:, :], moments[pair][:, :, 0], moments[pair][:, :, 0], ALU.mult)                    .then_inc(dve_e, 1)
                dve.scalar_tensor_tensor(t1[:, 0, :], c1[:, :], moments[pair][:, 0, 0:1], FO[:, 0, 0:D],
                                         ALU.mult, ALU.add).then_inc(dve_e, 1)
                dve.wait_ge(dve_e, own_base + 2)
                dve.scalar_tensor_tensor(ve_h[pair][:, :], moments[pair][:, :, 1], LN_EPS, msq[pair][:, :],
                                         ALU.add, ALU.subtract).then_inc(ve4, 1)
                dve.scalar_tensor_tensor(t1[:, 1, :], c1[:, :], moments[pair][:, 1, 0:1], FO[:, 1, 0:D],
                                         ALU.mult, ALU.add).then_inc(fo_read, 1)
                dve.wait_ge(dve_e, own_base + 3)
                dve.wait_ge(rs4, 2 * n + pair + 1)
                dve.scalar_tensor_tensor(o_t[:, 2 * pair, :], t1[:, 0, :], rs_h[pair][:, 0:1], x2c[:, 2 * pair, :],
                                         ALU.mult, ALU.add).then_inc(o_ready, 1)
                dve.wait_ge(fo_read, PRIME + 2 * n + pair + 1)
                dve.scalar_tensor_tensor(o_t[:, 2 * pair + 1, :], t1[:, 1, :], rs_h[pair][:, 1:2],
                                         x2c[:, 2 * pair + 1, :], ALU.mult, ALU.add).then_inc(o_ready, 1)
                dve.wait_ge(o_ready, TT * n + 2 * pair + 2)

            normalise(0)
            second_norm(0)
            low_parts(0)
            sum_squares(0, 0)
            with dve.Fori(1, NC) as n:
                normalise(n)
                sum_squares(n - 1, 1)
                finish(n - 1, 0)
                second_norm(n)
                low_parts(n)
                finish(n - 1, 1)
                sum_squares(n, 0)
            sum_squares(NC - 1, 1)
            finish(NC - 1, 0)
            finish(NC - 1, 1)

        @block.tensor
        def _(pe):
            prime(pe, PRIME, *pr_ready, *y_ready, fo_read)
            pe.wait_ge(const_ready, 6)
            pe.wait_ge(ctx_ld, 16 * B)
            for b in range(B):
                for k in range(KD):
                    m = b * KD + k
                    ins = pe.transpose(CT[:, m * MEM:(m + 1) * MEM], ctx_t[:, b, k * P:(k + 1) * P],
                                       ident[0:MEM, 0:MEM])
            ins.then_inc(ctx_full, 1)

            def turn_chunk(n):
                for tt in range(TT):
                    pe.wait_ge(xn_ready, TT * n + tt + 1)
                    for k in range(KD):
                        ins = pe.transpose(XT[:, k, tt * P:(tt + 1) * P], xn[:, tt, k * P:(k + 1) * P], ident[:, :])
                ins.then_inc(xT_full, 1)

            def queries_keys(n):
                pe.wait_ge(xT_evac, KD * n + KD)
                for m in range(2 * KD):
                    if not_first(n):
                        pe.wait_ge(r_ready, 2 * KD * (n - 1) + m + 1)
                    for k in range(KD):
                        ins = pe.matmul(QK[m], wqkv[:, k, m * P:(m + 1) * P], xnT[:, k, :],
                                        start=(k == 0), stop=(k == KD - 1))
                    ins.then_inc(qk_full, 1)

            def values(n, tiles):
                for tt in tiles:
                    if not_first(n) or tt >= 2:
                        pe.wait_ge(v_ready, TT * n + tt - 1)
                    for k in range(KD):
                        ins = pe.matmul(VV[tt % 2], xnT[:, k, tt * P:(tt + 1) * P], wqkv[:, k, 2 * D:3 * D],
                                        start=(k == 0), stop=(k == KD - 1))
                    ins.then_inc(v_full, 1)

            def turn_weights():
                for r in range(2 * KD):
                    k = r % KD
                    pe.wait_ge(tern_ready, 1 + (r >= KD))
                    if r < 2:
                        pe.wait_ge(r_ready, 2 * KD)
                    else:
                        pe.wait_ge(wt_read, r - 1)
                    for j in range(HJ):
                        src = tern_fcv[:, j, k * P:(k + 1) * P] if r < KD else tern_outv[:, k, j:H:HJ]
                        ins = pe.transpose(WT[r % 2][:, j * P:(j + 1) * P], src, identt[:, :])
                    ins.then_inc(wt_full, 1)

            def fold_norm():
                pe.wait_ge(w2_ready, 2)
                for which in range(2):
                    for j in range(HJ):
                        lhs, rhs = (ones[:, :], w2[:, j, 0:D]) if which == 0 else (lnb_wide[:, j, :], wT[:, j, :])
                        ins = pe.matmul(CC[which], lhs, rhs, start=(j == 0), stop=(j == HJ - 1))
                    ins.then_inc(cc_full, 1)

            turn_chunk(0)
            pe.wait_ge(qkvw_ld, 48)
            queries_keys(0)
            pe.wait_ge(abs_ready, 2)
            pe.matmul(VV[0][:, 0:2], mean_w[:, :], gam[:, 0:2], start=True, stop=True).then_inc(gam_full, 1)
            turn_weights()
            values(0, range(TT))
            turn_chunk(1)
            with pe.Fori(1, NC - 1) as n:
                queries_keys(n)
                values(n, range(TT))
                turn_chunk(n + 1)
            queries_keys(NC - 1)
            values(NC - 1, range(TT))

            def bank_wait(g, local):
                free = bank_free(g, local)
                if not_first(free):
                    pe.wait_ge(mx_read, free)

            def max_head(G, par, nu, h):
                qi, slot_, key, w = UNITS[nu]
                local = item(nu, h)
                bank_wait(G - 1, local)
                pe.matmul(MX[local % MXB][:, 0:w], stq_m[par][0:KR, h, qi * P:(qi + 1) * P],
                          stk_m[par][0:KR, h, key:key + w], start=True, stop=True).then_inc(mx_full, 1)

            def turn_rows(q, which, g):
                local = rows_item(which)
                wait_apart(pe, (mx_read, bank_free(g, local)), (mp_ready, q + 1))
                pe.transpose(MT[local % MXB], mparts[:, :, :].rearrange("p a r -> p (a r)"), identh[:, :])\
                    .then_inc(mx_full, 1)

            def slot(i, u, more):
                g = 2 * i + u
                pe.wait_ge(e_ld[u], 16 * 2 * (i + 1))
                pe.wait_ge(vs_ld[u], 16 * 2 * (i + 1))
                if more:
                    pe.wait_ge(m_ld[1 - u], 16 * 2 * LOADS * (occ(i, u + 1) + 1))

                def pv(s):
                    c, j, col, tok, w = STEPS[s]
                    rows = P if j < KB - 1 else LAST
                    if j == 0:
                        pe.wait_ge(y_ready[1 - c], PRIME + g + c)
                    for h in range(HG):
                        if h % 2 == 0:
                            if DIAG[s] is None:
                                pe.wait_ge(pr_ready[h // 2], PRIME + NS * g + s + 1)
                            else:
                                done = sum(d is not None for d in DIAG[:s + 1])
                                pe.wait_ge(sel_ready[h // 2], NDIAG * g + done)
                        ins = pe.matmul(ACC[32 * h:32 * h + 32, col:col + w], vst[u][0:rows, j, h, :],
                                        probs[(NS * u + s) % PB][0:rows, h, 0:w], start=(j == 0),
                                        stop=(s == CEND[c]), skip_group_check=True)
                    ins.then_inc(pv_done, 1)

                for s, (c, j, col, tok, w) in enumerate(STEPS):
                    rows = P if j < KB - 1 else LAST
                    if j == 0:
                        pe.wait_ge(mr_ld, 16 * (CB * g + c + 1))
                    if more:
                        max_head(g + 1, 1 - u, s, 0)
                    for k in range(2):
                        pe.wait_ge(pr_ready[k], PRIME + NS * g + s)
                        for h in (2 * k, 2 * k + 1):
                            ins = pe.matmul(SC[k][0:rows, h % 2, 0:w], stk_e[u][0:KM, h, j * P:j * P + rows],
                                            stq_e[u][0:KM, h, tok:tok + w], start=True, stop=True)
                            if h == 2 and more:
                                max_head(g + 1, 1 - u, s, 2)
                        ins.then_inc(sc_full[k], 1)
                        if more:
                            max_head(g + 1, 1 - u, s, 2 * k + 1)
                    if s >= LAG:
                        pv(s - LAG)
                    if s == ROWS_AT[0]:
                        turn_rows(CB * g + 1, 0, g)
                    if s == ROWS_AT[1] and more:
                        turn_rows(CB * g + 2, 1, g)
                for s in range(NS - LAG, NS):
                    pv(s)

            pe.wait_ge(m_ld[0], 16 * 2 * LOADS)
            pe.wait_ge(v_ready, TT * NC)
            for nu in range(NU):
                for h in range(HG):
                    max_head(0, 0, nu, h)
                if nu == ROWS_AT[1]:
                    turn_rows(0, 1, -1)
                if nu == UA + 2:
                    fold_norm()
            pe.wait_ge(cc_read, 2)
            pe.wait_ge(ones_ready, 6)
            with pe.Fori(0, NG // 2 - 1) as i:
                slot(i, 0, True)
                slot(i, 1, True)
            slot(NG // 2 - 1, 0, True)
            slot(NG // 2 - 1, 1, False)

            pe.wait_ge(late_ld, 32)
            pe.wait_ge(y_ready[1], PRIME + NG)

            def turn_attention(n):
                pe.wait_ge(c_ld, 16 * n + 16)
                if not_first(n):
                    pe.wait_ge(lo_ready, KD * n)
                for tt in range(TT):
                    for gg in range(GB):
                        ins = pe.transpose(YT[tt // 2][:, tt % 2, gg * P:(gg + 1) * P],
                                           yraw[:, gg, tt * P:(tt + 1) * P], ident[:, :])
                    if tt % 2 == 1:
                        ins.then_inc(yt_full, 1)

            def turn_features(n):
                for tt in range(TT):
                    if tt % 2 == 0:
                        pe.wait_ge(yn_ready, 2 * n + tt // 2 + 1)
                    for k in range(KD):
                        ins = pe.transpose(AT[:, k, tt * P:(tt + 1) * P], yn[:, tt, k * P:(k + 1) * P], ident[:, :])
                ins.then_inc(at_full, 1)

            def project(n):
                pe.wait_ge(ynT_ready, KD * n + KD)
                if not_first(n):
                    pe.wait_ge(gel_ready, HJ * n)
                for tt in range(TT):
                    for k in range(KD):
                        ins = pe.matmul(FC[tt // 2][:, (tt % 2) * D:(tt % 2 + 1) * D], ynT[:, k, tt * P:(tt + 1) * P],
                                        wpr[:, k, :], start=(k == 0), stop=(k == KD - 1), skip_group_check=True)
                    if tt % 2 == 1:
                        ins.then_inc(pj_full, 1)

            def turn_norm(n):
                for tt in range(TT):
                    pe.wait_ge(xn3, TT * n + tt + 1)
                    for k in range(KD):
                        ins = pe.transpose(LN[:, k, tt * P:(tt + 1) * P], xn[:, tt, k * P:(k + 1) * P], ident[:, :])
                ins.then_inc(ln_full, 1)

            def hidden(n):
                pe.wait_ge(hi_ready, KD * n + KD)
                pe.wait_ge(lo_ready, KD * n + KD)
                for j in range(HJ):
                    if j >= 2:
                        pe.wait_ge(gel_ready, HJ * n + j - 1)
                    for k in range(KD):
                        for part in (hi, lo):
                            ins = pe.matmul(FC[j % 2], fcT[:, k, j, :], part[:, k, :],
                                            start=(k == 0 and part is hi), stop=(k == KD - 1 and part is lo))
                    ins.then_inc(fc_full, 1)

            def second(n, tt):
                if tt == 0:
                    pe.wait_ge(gel_ready, HJ * n + HJ)
                if tt % 2 == 0:
                    pe.wait_ge(fo_read, PRIME + 2 * n + tt // 2)
                for j in range(HJ):
                    pe.matmul(FO[:, tt % 2, 0:D + 1], gel[j][:, tt * P:(tt + 1) * P], w2[:, j, 0:D + 1],
                              start=(j == 0), stop=(j == HJ - 1), skip_group_check=True)

            def mean_squares(n, pair):
                if pair == 0:
                    pe.wait_ge(ssq_ready, 2 * n + 2)
                for t in range(2):
                    tt = 2 * pair + t
                    for half, part in enumerate((ssq, ssq2)):
                        ins = pe.matmul(FO[:, t, D + 1:D + 2], part[:, tt * P:(tt + 1) * P], w2[:, 0, D:D + 1],
                                        start=False, stop=(half == 1), skip_group_check=True)
                ins.then_inc(fo_full, 1)

            turn_attention(0)
            turn_features(0)
            project(0)
            turn_norm(0)
            hidden(0)
            with pe.Fori(1, NC) as n:
                turn_attention(n)
                second(n - 1, 0)
                turn_features(n)
                second(n - 1, 1)
                mean_squares(n - 1, 0)
                project(n)
                second(n - 1, 2)
                second(n - 1, 3)
                mean_squares(n - 1, 1)
                turn_norm(n)
                hidden(n)
            for pair in range(2):
                second(NC - 1, 2 * pair)
                second(NC - 1, 2 * pair + 1)
                mean_squares(NC - 1, pair)


_INS = ["x", "ctx_1024", "L0_xattn_W_attn", "L0_xattn_b_attn", "L0_xattn_W_proj", "L0_xattn_b_proj",
        "L0_ffn_W_fc", "L0_ffn_ln_w", "L0_ffn_ln_b", "L0_ffn_W_proj"]


def kernel(**inputs):
    import numpy as _np
    import concourse.bacc as _bacc
    from concourse import mybir as _mybir
    from concourse.bass_utils import run_bass_kernel_spmd as _run

    nc = _bacc.Bacc("TRN2", target_bir_lowering=False, num_devices=1)
    arrays, args = {}, []
    for name in _INS:
        a = _np.ascontiguousarray(inputs[name])
        arrays[f"in_{name}"] = a
        args.append(nc.dram_tensor(f"in_{name}", a.shape, _mybir.dt.from_np(a.dtype), kind="ExternalInput").ap())
    args.append(nc.dram_tensor("out_0", (B, T, D), F32, kind="ExternalOutput").ap())
    build(nc, *args)
    r = _run(nc, [arrays], core_ids=[0])
    return r.results[0]["out_0"]
```

```python
from contextlib import ExitStack

import concourse.bass as bass
from concourse import mybir

F32 = mybir.dt.float32
BF16 = mybir.dt.bfloat16
F16 = mybir.dt.float16
ALU = mybir.AluOpType
ACT = mybir.ActivationFunctionType
AX = mybir.AxisListType

B, T, D = 2, 1024, 256
MEM = 77
NH, HD = 16, 16
H = 1024
P = 128
KD = D // P
HG = 4
GB = NH // HG
NG = B * GB
S = MEM + T
KB = -(-S // P)
LAST = S - (KB - 1) * P
SP = 1104
CH = 512
NC = B * T // CH
CB = T // CH
TT = CH // P
HJ = H // P
LN_EPS = 1e-5
TERN_EPS = 1e-6
BIG = -1e30
LOWEST = -3.0e38
PAIRS = [(0, 0), (0, 1), (0, 2), (1, 0), (1, 1), (2, 0)]
KR = len(PAIRS) * HD
KM = KR + 3

BLOCKS = [[0, 3, 1, 2, 4], [0, 7, 1, 6, 2, 5, 3, 4, 8]]
STEPS = []
for _c in range(CB):
    for _j in BLOCKS[_c]:
        _lo = max(_c * CH, _j * P - MEM)
        STEPS.append((_c, _j, _lo - _c * CH, _lo, (_c + 1) * CH - _lo))
    assert sorted(BLOCKS[_c]) == [j for j in range(KB) if j * P - MEM < (_c + 1) * CH]
NS = len(STEPS)
CEND = [max(s for s, st in enumerate(STEPS) if st[0] == c) for c in range(CB)]
DIAG = []
for _c, _j, _col, _tok, _w in STEPS:
    _a, _b = max(_tok, _j * P - MEM), min(_tok + _w, _j * P - MEM + P)
    DIAG.append((_a - _tok, _b - _a) if _b > _a else None)
NDIAG = sum(d is not None for d in DIAG)
UNITS = []
for _c in range(CB):
    _u = []
    for _i in range(_c * TT, (_c + 1) * TT):
        _n = MEM + P * (_i + 1)
        _u += [(_i, _s, _s * CH, min(CH, _n - _s * CH)) for _s in range(-(-_n // CH))]
    _u.sort(key=lambda u: -u[3])
    _steps = sorted((n for n, st in enumerate(STEPS) if st[0] == _c), key=lambda n: (-STEPS[n][4], n))
    _mine = dict(zip(_steps, _u))
    UNITS += [_mine[n] for n in sorted(_mine)]
NU = len(UNITS)
assert NU == NS
UA = sum(u[0] < TT for u in UNITS)
MSLOTS = max(u[1] for u in UNITS) + 1
LOADS = len(PAIRS)
MXB = 3
ROWS_AT = (0, UA + 1)
ITEMS = HG * NU + 2
BIAS_AT = next(s for s in range(CEND[0] + 1, NS) if DIAG[s])
FOLD_AT = HG * UA


def item(nu, h):
    return HG * nu + h + sum(nu > at for at in ROWS_AT)


def rows_item(which):
    return HG * (ROWS_AT[which] + 1) + which


PRIME, DMA_PRIME = 1, 16
PB = 4
LAG = 2


def build(nc, x, ctx_in, w_attn, b_attn, w_proj, b_proj, w_fc, ln_w, ln_b, w_out, out):
    q_scr = nc.dram_tensor("q_scr", [NG, HG, HD, 3, T], BF16).ap()
    k_scr = nc.dram_tensor("k_scr", [NG, HG, HD, 3, SP], BF16).ap()
    v_scr = nc.dram_tensor("v_scr", [NG, KB * P, 2 * HG * HD], F32).ap()
    y_scr = nc.dram_tensor("y_scr", [B, GB, P, T], F32).ap()
    r_scr = nc.dram_tensor("r_scr", [B, NH, T], F32).ap()
    m_scr = nc.dram_tensor("m_scr", [3, HG * TT, P], BF16).ap()
    q_st = q_scr.rearrange("(m g) h d a t -> m (g h d) a t", g=2)
    k_st = k_scr.rearrange("(m g) h d a t -> m (g h d) a t", g=2)
    v_st_view = v_scr.rearrange("(b g) s d -> b s g d", g=GB)
    x_ch = x.rearrange("b (c i p) d -> (b c) p i d", i=TT, p=P)
    out_ch = out.rearrange("b (c i p) d -> (b c) p i d", i=TT, p=P)

    with ExitStack() as es:
        def sb(name, shape, dt=F32):
            return es.enter_context(nc.sbuf_tensor(name, shape, dt))

        def sem(name):
            return es.enter_context(nc.semaphore(name))

        def sems(name, n):
            return [sem(f"{name}{i}") for i in range(n)]

        ps = es.enter_context(nc.psum_tensor("ps", [P, 8, CH], F32))

        ident = sb("ident", [P, P])
        identh = sb("identh", [P, P], BF16)
        identt = sb("identt", [P, P], F16)
        ones = sb("ones", [P, P])
        mean_w = sb("mean_w", [P, P])
        nhalf = sb("nhalf", [P, TT])
        wqkv = sb("wqkv", [P, KD, 3 * D])
        wpr = sb("wpr", [P, KD, D])
        bqk = sb("bqk", [P, 2 * KD])
        bv = sb("bv", [P, D])
        bpr = sb("bpr", [P, D])
        lnw = sb("lnw", [P, HJ])
        lnb = sb("lnb", [P, HJ])
        fcT = sb("fcT", [P, KD, HJ, P], F16)
        w2 = sb("w2", [P, HJ, D + 2])
        c1 = sb("c1", [P, D])
        c2 = sb("c2", [P, D])
        gam = sb("gam", [P, 8])
        stq_m = [sb(f"stq_m{i}", [P, HG, T], BF16) for i in range(2)]
        stk_m = [sb(f"stk_m{i}", [P, HG, SP], BF16) for i in range(2)]
        stq_e = [sb(f"stq_e{i}", [P, HG, T], BF16) for i in range(2)]
        stk_e = [sb(f"stk_e{i}", [P, HG, SP], BF16) for i in range(2)]
        vst = [sb(f"vst{i}", [P, KB, HG, 2 * HD]) for i in range(2)]
        probs = [sb(f"probs{i}", [P, HG, CH]) for i in range(PB)]
        window = sb("window", [P, S], BF16)
        junk = [sb(f"junk{i}", [P, CH], BF16) for i in range(MXB)]
        mpart = [sb(f"mpart{i}", [P, HG, TT, MSLOTS]) for i in range(CB)]
        negm = sb("negm", [P, HG * TT])
        mres = sb("mres", [P, HG * TT])
        mparts = sb("mparts", [P, 3, HG * TT], BF16)
        mrows = sb("mrows", [3 * HG * TT, P], BF16)
        ystage = [sb(f"ystage{i}", [P, CH]) for i in range(CB)]
        raw_fc = stk_m[0][:, :, :].rearrange("p h s -> p (h s)")[:, 0:2 * HJ * D].bitcast(F32)
        raw_fc = raw_fc.rearrange("p (j d) -> p j d", d=D)
        raw_out = stk_m[1][:, :, :].rearrange("p h s -> p (h s)")[:, 0:2 * KD * H].bitcast(F32)
        raw_out = raw_out.rearrange("p (k h) -> p k h", h=H)
        tern_a = probs[0][:, :, :].rearrange("p h t -> p (h t)").bitcast(F16)[:, 0:HJ * D]
        tern_b = probs[1][:, :, :].rearrange("p h t -> p (h t)").bitcast(F16)
        tern_fcv = tern_b[:, 0:HJ * D].rearrange("p (j d) -> p j d", d=D)
        tern_outv = tern_b[:, HJ * D:2 * HJ * D].rearrange("p (k h) -> p k h", h=H)
        wT = probs[0][:, :, :].rearrange("p h t -> p (h t)")[:, 0:HJ * D].rearrange("p (j d) -> p j d", d=D)
        lnb_wide = probs[1][:, :, :].rearrange("p h t -> p (h t)")[:, 0:HJ * P].rearrange("p (j m) -> p j m", m=P)
        x_a = sb("x_a", [P, TT, D])
        xn = sb("xn", [P, TT, D])
        xnT = sb("xnT", [P, KD, CH])
        stats = sb("stats", [P, TT, 6])
        mv = sb("mv", [P, TT, 2])
        ve = sb("ve", [P, TT])
        rs = sb("rs", [P, TT])
        late_parts = probs[2][:, :, :].rearrange("p h t -> p (h t)").bitcast(BF16)
        parts = [sb(f"parts{i}", [P, 3, CH], BF16) for i in range(2)]
        parts += [late_parts[:, i * 3 * CH:(i + 1) * 3 * CH].rearrange("p (a t) -> p a t", t=CH) for i in range(2)]
        resid = [sb(f"resid{i}", [P, CH]) for i in range(2)] + [probs[3][:, i, :] for i in range(2)]
        vtile = sb("vtile", [P, TT, NH, 2 * HD])
        vctx = sb("vctx", [MEM, B, NH, 2 * HD])
        ctx_t = sb("ctx_t", [MEM, B, D])
        ctx_p = sb("ctx_p", [P, 3, B * KD, MEM], BF16)
        ctx_r = sb("ctx_r", [P, B * KD * MEM])
        den = [sb(f"den{i}", [P, NH * T // P]) for i in range(B)]
        rden = [sb(f"rden{i}", [P, NH * T // P]) for i in range(B)]

        def room(t, first, shape, dt=F32):
            v = t[:, :, :].rearrange("p a b -> p (a b)").bitcast(F32)
            a, b = shape
            words = a * b // (1 if dt == F32 else 2)
            v = v[:, first:first + words]
            return (v if dt == F32 else v.bitcast(dt)).rearrange("p (a b) -> p a b", b=b)

        yraw = room(stq_m[0], 0, (KD, CH))
        ynT = room(stq_m[0], KD * CH, (KD, CH))
        rwide = room(stq_m[1], 0, (KD, CH))
        xb = room(stk_m[0], 0, (TT, D))
        x2 = room(stk_m[0], TT * D, (TT, D))
        x2c = room(stk_m[1], 0, (TT, D))
        o_t = room(stk_m[1], TT * D, (TT, D))
        hi = room(stq_e[1], 0, (KD, CH), F16)
        lo = room(stq_e[1], KD * CH // 2, (KD, CH), F16)
        g_lo = stk_e[0][:, :, :].rearrange("p h s -> p (h s)")[:, 0:HJ * CH].bitcast(F32)
        g_hi = stq_e[0][:, :, :].rearrange("p h s -> p (h s)")[:, 0:HJ * CH].bitcast(F32)
        gel = [(g_lo if j < HJ // 2 else g_hi)[:, (j % (HJ // 2)) * CH:(j % (HJ // 2) + 1) * CH] for j in range(HJ)]
        sq = probs
        halves = [sb(f"halves{i}", [P, CH]) for i in range(2)]
        ssq = sb("ssq", [P, CH])
        moments = [sb(f"moments{i}", [P, 2, 2]) for i in range(2)]
        msq = [sb(f"msq{i}", [P, 2]) for i in range(2)]
        ve_h = [sb(f"ve_h{i}", [P, 2]) for i in range(2)]
        rs_h = [sb(f"rs_h{i}", [P, 2]) for i in range(2)]
        t1 = sb("t1", [P, 2, D])

        fc_ld, wo_ld, small_ld, qkvw_ld = sem("fc_ld"), sem("wo_ld"), sem("small_ld"), sem("qkvw_ld")
        late_ld, ctx_ld = sem("late_ld"), sem("ctx_ld")
        dve_w, dve_a, dve_b, pool_own = sem("dve_w"), sem("dve_a"), sem("dve_b"), sem("pool_own")
        const_ready, ones_ready = sem("const_ready"), sem("ones_ready")
        abs_ready, gam_full = sem("abs_ready"), sem("gam_full")
        tern_ready, wt_full, wt_read = sem("tern_ready"), sem("wt_full"), sem("wt_read")
        w2_ready, cc_full, cc_read = sem("w2_ready"), sem("cc_full"), sem("cc_read")
        ctx_full, ctx_p1, ctx_p2, ctx_p3 = sem("ctx_full"), sem("ctx_p1"), sem("ctx_p2"), sem("ctx_p3")
        ctx_st, vctx_ready = sem("ctx_st"), sem("vctx_ready")
        x_ld = sem("x_ld")
        ve_ready, rs_ready, xn_ready = sem("ve_ready"), sem("rs_ready"), sem("xn_ready")
        xT_full, xT_evac = sem("xT_full"), sem("xT_evac")
        qk_full, p1_ready, p2_ready, p3_ready = sem("qk_full"), sem("p1_ready"), sem("p2_ready"), sem("p3_ready")
        r_ready, v_full, v_ready = sem("r_ready"), sem("v_full"), sem("v_ready")
        qk_st, v_st = sems("qk_st", 2 * KD), sems("v_st", TT)
        m_ld = sems("m_ld", 2)
        e_ld = sems("e_ld", 2)
        vs_ld = sems("vs_ld", 2)
        mx_full, mx_read, mp_ready = sem("mx_full"), sem("mx_read"), sem("mp_ready")
        mr_st, mr_ld = sem("mr_st"), sem("mr_ld")
        sc_full, pr_ready, sel_ready = sems("sc_full", 2), sems("pr_ready", 2), sems("sel_ready", 2)
        pv_done = sem("pv_done")
        y_ready, y_st = sems("y_ready", CB), sems("y_st", CB)
        c_ld, x3_ld, xb_ready = sem("c_ld"), sem("x3_ld"), sem("xb_ready")
        den_ld, rden_ready, rden_st, ynT_ready = sem("den_ld"), sem("rden_ready"), sem("rden_st"), sem("ynT_ready")
        pj_full, x2_ready, dve_x, x2c_ready = sem("pj_full"), sem("x2_ready"), sem("dve_x"), sem("x2c_ready")
        ve3, rs3, xn3, ln_full = sem("ve3"), sem("rs3"), sem("xn3"), sem("ln_full")
        hi_ready, lo_ready = sem("hi_ready"), sem("lo_ready")
        fc_full, gel_ready, sq_ready, ssq_ready = sem("fc_full"), sem("gel_ready"), sems("sq_ready", 2), sem("ssq_ready")
        ssq_sum = sem("ssq_sum")
        fo_full, fo_read, dve_e, ve4, rs4 = sem("fo_full"), sem("fo_read"), sem("dve_e"), sem("ve4"), sem("rs4")
        o_ready, o_st = sem("o_ready"), sem("o_st")

        XT = ps[:, 0:2, :]
        QK = [ps[:, 2, :], ps[:, 3, :], ps[:, 6, :], ps[:, 7, :]]
        VV = [ps[:, 4, 0:D], ps[:, 5, 0:D]]
        CT = ps[:, 6, 0:B * KD * MEM]
        WT = [ps[:, 6, :].bitcast(F16), ps[:, 7, :].bitcast(F16)]
        GAM = ps[:, 0, 0:1]
        CC = [ps[:, 0, 0:D], ps[:, 1, 0:D]]
        SC = [ps[:, 0:2, :], ps[:, 2:4, :]]
        MX = [ps[:, b, :] for b in (4, 5, 7)]
        ACC = ps[:, 6, :]
        MT = [mx[0:3 * HG * TT, 0:P // 2].bitcast(BF16) for mx in MX]
        LN = ps[:, 2:4, :]
        LN0 = ps[:, 4:6, :]
        FC = [ps[:, 4, :], ps[:, 5, :]]
        FO = ps[:, 6:8, :]

        block = es.enter_context(nc.Block())

        def not_first(n):
            return not isinstance(n, int) or n > 0

        def prime(eng, value, *signals):
            for signal in signals:
                eng.sem_inc(signal, value)

        def wait_apart(eng, *waits):
            waits = [(signal, count if isinstance(count, int) else eng.to_reg(count)) for signal, count in waits]
            eng.wait_ge(const_ready, 6)
            for signal, count in waits:
                eng.wait_ge(signal, count)

        def items_before(g, local):
            if isinstance(g, int) and g == -1 and local <= rows_item(0):
                return local
            if isinstance(g, int) and g == NG - 1:
                local -= HG * (ROWS_AT[0] + 1)
            return ITEMS * (g + 1) + local - 1

        def bank_free(g, local):
            earlier = local - MXB
            if earlier >= 0:
                return items_before(g, earlier) + 1
            if isinstance(g, int) and g == -1:
                return 0
            return items_before(g - 1, max(k for k in range(ITEMS) if k % MXB == local % MXB)) + 1

        def wait_all(eng, *waits):
            waits = [(sig, count if isinstance(count, int) else eng.to_reg(count)) for sig, count in waits]
            for signal, count in waits:
                eng.wait_ge(signal, count)

        def occ(i, off):
            return i + off // 2

        @block.sync
        def _(sp):
            prime(sp, PRIME, *sc_full)
            def load_x(n):
                if not_first(n):
                    sp.wait_ge(xn_ready, TT * n)
                sp.dma_start(x_a[:, :, :], x_ch[n]).then_inc(x_ld, 16)

            for b in range(B):
                sp.dma_start(ctx_t[:, b, :], ctx_in[b]).then_inc(ctx_ld, 16)
            load_x(0)
            sp.dma_start(wqkv[:, :, :], w_attn.rearrange("(k p) n -> p k n", p=P)).then_inc(qkvw_ld, 16)
            sp.dma_start(bqk[:, :], b_attn[0:2 * D].rearrange("(m p) -> p m", p=P),
                         allow_slow_non_contiguous=True).then_inc(qkvw_ld, 16)
            sp.dma_start(bv[:, :], b_attn[2 * D:3 * D].partition_broadcast(P)).then_inc(qkvw_ld, 16)
            sp.dma_start(raw_fc, w_fc.rearrange("(p j) d -> p j d", j=HJ)).then_inc(fc_ld, 16)
            sp.dma_start(raw_out, w_out.rearrange("(k p) h -> p k h", p=P)).then_inc(wo_ld, 16)
            load_x(1)
            sp.dma_start(lnw[:, :], ln_w.rearrange("(p j) -> p j", j=HJ)).then_inc(small_ld, 16)
            sp.dma_start(lnb[:, :], ln_b.rearrange("(p j) -> p j", j=HJ)).then_inc(small_ld, 16)
            sp.dma_start(wpr[:, :, :], w_proj.rearrange("(k p) n -> p k n", p=P)).then_inc(late_ld, 16)
            sp.dma_start(bpr[:, :], b_proj.partition_broadcast(P)).then_inc(late_ld, 16)
            sp.wait_ge(vctx_ready, 2)
            for b in range(B):
                sp.dma_start(v_st_view[b, 0:MEM], vctx[:, b, :, :].rearrange("p (g h) d -> p g (h d)", g=GB))\
                    .then_inc(ctx_st, 16)
            for a, part_ready in enumerate((ctx_p1, ctx_p2, ctx_p3)):
                sp.wait_ge(part_ready, 1)
                sp.dma_start(k_st[:, :, a, 0:MEM].rearrange("m r t -> r m t"), ctx_p[:, a, :, :]).then_inc(ctx_st, 16)

            q_tiles = q_st.rearrange("(b k) r a (c t) -> b c k r a t", k=KD, c=CB)
            k_tiles = k_st[:, :, :, MEM:S].rearrange("(b k) r a (c t) -> b c k r a t", k=KD, c=CB)
            v_tiles = v_st_view[:, MEM:S].rearrange("b (c i p) g d -> b c i p g d", i=TT, p=P)

            def store_chunk(n, more):
                for m in range(2 * KD):
                    sp.wait_ge(p3_ready, 2 * KD * n + m + 1)
                    dst = (q_tiles if m < KD else k_tiles)[n // CB, n % CB, m % KD]
                    sp.dma_start(dst, parts[m][:, :, :]).then_inc(qk_st[m], 16)
                    if m == 1 and more:
                        load_x(n + 2)
                for tt in range(TT):
                    sp.wait_ge(v_ready, TT * n + tt + 1)
                    sp.dma_start(v_tiles[n // CB, n % CB, tt],
                                 vtile[:, tt, :, :].rearrange("p (g h) d -> p g (h d)", g=GB)).then_inc(v_st[tt], 16)

            def stored(chunks):
                for done in qk_st + v_st:
                    sp.wait_ge(done, 16 * chunks)

            def load_stack(q_dst, k_dst, g, done):
                for r, (qa, ka) in enumerate(PAIRS):
                    rows = slice(r * HD, (r + 1) * HD)
                    sp.dma_start(q_dst[rows, :, :], q_scr[g, :, :, qa, :].rearrange("h d t -> d h t")).then_inc(done, 16)
                    sp.dma_start(k_dst[rows, :, 0:S], k_scr[g, :, :, ka, 0:S].rearrange("h d t -> d h t"))\
                        .then_inc(done, 16)

            def load_values(v_dst, g, done):
                sp.dma_start(v_dst[:, 0:KB - 1, :, :].rearrange("p j h d -> p j (h d)"),
                             v_scr[g, 0:(KB - 1) * P, :].rearrange("(j p) d -> p j d", p=P)).then_inc(done, 16)
                sp.dma_start(v_dst[0:LAST, KB - 1, :, :].rearrange("p h d -> p (h d)"),
                             v_scr[g, (KB - 1) * P:S, :]).then_inc(done, 16)

            def copy_stack(par, loads, *before):
                wait_all(sp, *before, (m_ld[par], 16 * 2 * LOADS * loads))
                sp.dma_start(stq_e[par][0:KR, :, :], stq_m[par][0:KR, :, :]).then_inc(e_ld[par], 16)
                sp.dma_start(stk_e[par][0:KR, :, 0:S], stk_m[par][0:KR, :, 0:S]).then_inc(e_ld[par], 16)

            def place_max_rows(par, c, q, g):
                sp.wait_ge(mx_read, items_before(g, rows_item(1 - c)) + 1)
                sp.dma_start(m_scr.rearrange("a r t -> (a r) t"), mrows[:, :]).then_inc(mr_st, 16)
                sp.wait_ge(mr_st, 16 * q + 16)
                sp.dma_start(stq_e[par][KR:KM, :, c * CH:(c + 1) * CH],
                             m_scr.rearrange("a (h i) t -> a h (i t)", h=HG)).then_inc(mr_ld, 16)

            with sp.Fori(0, NC - 2) as n:
                store_chunk(n, True)
            assert CB == 2 and NC == B * CB
            stored(CB)
            sp.wait_ge(ctx_st, 16 * (B + 3))
            sp.wait_ge(tern_ready, 1)
            load_stack(stq_m[0], stk_m[0], 0, m_ld[0])
            with sp.Fori(NC - 2, NC) as n:
                store_chunk(n, False)
            sp.wait_ge(tern_ready, 2)
            load_stack(stq_m[1], stk_m[1], 1, m_ld[1])
            load_values(vst[0], 0, vs_ld[0])
            copy_stack(0, 1)
            stored(NC)
            place_max_rows(0, 0, 0, -1)

            heads = y_scr.rearrange("b g (h r) t -> b (g h) r t", r=2 * HD)
            values_of = heads[:, :, 0:HD, :].rearrange("b (k h) r (c t) -> b c k h r t", k=KD, c=CB)
            wide_of = r_scr.rearrange("b (k h o) (c t) -> b c k h o t", k=KD, o=1, c=CB)

            def invert(b):
                sp.dma_start(den[b][:, :], heads[b, :, HD, :].rearrange("h (x t) -> h x t", t=P)).then_inc(den_ld, 16)
                sp.wait_ge(rden_ready, b + 1)
                sp.dma_start(r_scr[b].rearrange("h (x t) -> (h x) t", t=P), rden[b][:, :]).then_inc(rden_st, 16)
                sp.wait_ge(rden_st, 16 * b + 16)

            def load_chunk(n):
                if not_first(n):
                    sp.wait_ge(ynT_ready, n)
                for k in range(KD):
                    sp.dma_start(yraw[:, k, :], values_of[n // CB, n % CB, k]).then_inc(c_ld, 16)
                    sp.dma_start(rwide[:, k, :], wide_of[n // CB, n % CB, k].to_broadcast([NH // KD, HD, CH]))\
                        .then_inc(c_ld, 16)
                if not_first(n):
                    sp.wait_ge(xb_ready, n)
                sp.dma_start(x_a[:, :, :], x_ch[n]).then_inc(x3_ld, 16)

            def slot(i, u, more_m, more_e):
                g = 2 * i + u
                place_max_rows(u, 1, 2 * g + 1, g)
                if not more_m and more_e:
                    for c in range(CB):
                        sp.wait_ge(y_st[c], DMA_PRIME + 16 * GB)
                    invert(0)
                if not more_e:
                    sp.wait_ge(mx_full, ITEMS * NG - 1)
                    sp.wait_ge(e_ld[u], 16 * 2 * (i + 1))
                    load_chunk(0)
                if more_e:
                    copy_stack(1 - u, occ(i, u + 1) + 1, (sc_full[1], PRIME + NS * g))
                if more_m:
                    wait_all(sp, (mx_full, items_before(g, 0)), (e_ld[u], 16 * 2 * (i + 1)))
                    load_stack(stq_m[u], stk_m[u], g + 2, m_ld[u])
                if more_e:
                    sp.wait_ge(pv_done, PB + NS * g)
                    load_values(vst[1 - u], g + 1, vs_ld[1 - u])
                sp.wait_ge(y_ready[0], PRIME + g + 1)
                sp.dma_start(y_scr[g // GB, g % GB, :, 0:CH], ystage[0][:, :]).then_inc(y_st[0], 16)
                if more_e:
                    place_max_rows(1 - u, 0, 2 * g + 2, g)
                else:
                    load_chunk(1)
                sp.wait_ge(y_ready[1], PRIME + g + 1)
                sp.dma_start(y_scr[g // GB, g % GB, :, CH:T], ystage[1][:, :]).then_inc(y_st[1], 16)

            with sp.Fori(0, NG // 2 - 1) as i:
                slot(i, 0, True, True)
                slot(i, 1, True, True)
            slot(NG // 2 - 1, 0, False, True)
            slot(NG // 2 - 1, 1, False, False)

            for c in range(CB):
                sp.wait_ge(y_st[c], DMA_PRIME + 16 * NG)
            invert(1)
            def store(n):
                sp.wait_ge(o_ready, TT * n + TT)
                sp.dma_start(out_ch[n], o_t[:, :, :]).then_inc(o_st, 16)

            with sp.Fori(2, NC) as n:
                load_chunk(n)
                store(n - 2)
            store(NC - 2)
            store(NC - 1)
            sp.wait_ge(o_st, DMA_PRIME + 16 * NC)

        @block.gpsimd
        def _(pool):
            for t in (ident, identh, identt):
                pool.memset(t[:, :], 0.0).then_inc(pool_own, 1)
            pool.memset(window[:, :], 0.0).then_inc(pool_own, 1)
            pool.wait_ge(pool_own, 4)
            for t in (ident, identh, identt):
                pool.affine_select(out=t[:, :], in_=t[:, :], compare_op=ALU.not_equal, fill=1.0, base=0,
                                   pattern=[[-1, P]], channel_multiplier=1).then_inc(const_ready, 1)
            pool.affine_select(out=window[:, S - P:S], in_=window[:, S - P:S], compare_op=ALU.is_ge, fill=BIG,
                               base=0, pattern=[[-1, P]], channel_multiplier=1).then_inc(const_ready, 1)
            pool.memset(ones[:, :], 1.0).then_inc(const_ready, 1)
            pool.memset(nhalf[:, :], -0.5).then_inc(pool_own, 1)
            pool.memset(mean_w[:, :], 1.0 / (H * D)).then_inc(const_ready, 1)
            pool.memset(vtile[:, :, :, HD:2 * HD].rearrange("p i h d -> p (i h) d"), 1.0).then_inc(ones_ready, 1)
            pool.memset(vctx[:, :, :, HD:2 * HD], 1.0).then_inc(vctx_ready, 1)
            for c in range(CB):
                pool.memset(mpart[c][:, :, :, :], LOWEST).then_inc(ones_ready, 1)
            pool.memset(w2[:, :, D:D + 2], 1.0 / H).then_inc(ones_ready, 1)
            pool.wait_ge(pool_own, 5)
            pool.wait_ge(ctx_p2, 1)
            pool.tensor_tensor(ctx_p[:, 2, :, :].rearrange("p m t -> p (m t)"), ctx_r[:, :],
                               ctx_p[:, 1, :, :].rearrange("p m t -> p (m t)"), ALU.subtract).then_inc(ctx_p3, 1)
            def token_deviations(n):
                pool.wait_ge(ve_ready, n + 1)
                pool.tensor_tensor(rs[:, :], ve[:, :], nhalf[:, :], ALU.pow).then_inc(rs_ready, 1)

            def third_parts(n):
                for m in range(2 * KD):
                    pool.wait_ge(p2_ready, 2 * KD * n + m + 1)
                    pool.tensor_tensor(parts[m][:, 2, :], resid[m][:, :], parts[m][:, 1, :],
                                       ALU.subtract).then_inc(p3_ready, 1)

            token_deviations(0)
            with pool.Fori(0, NC - 1) as n:
                token_deviations(n + 1)
                third_parts(n)
            third_parts(NC - 1)
            pool.wait_ge(small_ld, 32)
            pool.wait_ge(wt_read, 2 * KD)
            pool.tensor_tensor(w2[:, :, 0:D], wT, lnw[:, :].rearrange("p (j o) -> p j o", o=1).to_broadcast([P, HJ, D]),
                               ALU.mult).then_inc(w2_ready, 1)
            pool.tensor_copy(lnb_wide, lnb[:, :].rearrange("p (j o) -> p j o", o=1).to_broadcast([P, HJ, P]))\
                .then_inc(w2_ready, 1)

            def with_bias(n):
                pool.wait_ge(x3_ld, 16 * n + 16)
                if not_first(n):
                    pool.wait_ge(x2_ready, 2 * n)
                pool.tensor_tensor(xb[:, :, :], x_a[:, :, :],
                                   bpr[:, :].rearrange("p (o d) -> p o d", o=1).to_broadcast([P, TT, D]),
                                   ALU.add).then_inc(xb_ready, 1)

            def slot(i, u, last=False):
                g = 2 * i + u
                for s, (c, j, col, tok, w) in enumerate(STEPS):
                    if DIAG[s] is None:
                        continue
                    a, dw = DIAG[s]
                    rows = P if j < KB - 1 else LAST
                    for k in range(2):
                        wait_apart(pool, (pr_ready[k], PRIME + NS * g + s + 1))
                        part = probs[(NS * u + s) % PB][0:rows, 2 * k:2 * k + 2, a:a + dw]
                        pool.affine_select(out=part, in_=part, compare_op=ALU.is_ge, fill=0.0,
                                           base=tok + a + MEM - P * j, pattern=[[0, 2], [1, dw]],
                                           channel_multiplier=-1).then_inc(sel_ready[k], 1)
                    if last and s == BIAS_AT:
                        pool.wait_ge(late_ld, 32)
                        with_bias(0)

            with pool.Fori(0, NG // 2 - 1) as i:
                slot(i, 0)
                slot(i, 1)
            slot(NG // 2 - 1, 0)
            slot(NG // 2 - 1, 1, last=True)

            pool.wait_ge(cc_read, 2)

            def deviations(n):
                pool.wait_ge(ve3, n + 1)
                pool.tensor_tensor(rs[:, :], ve[:, :], nhalf[:, :], ALU.pow).then_inc(rs3, 1)

            def hidden_deviations(n, pair):
                pool.wait_ge(ve4, 2 * n + pair + 1)
                pool.tensor_tensor(rs_h[pair][:, :], ve_h[pair][:, :], nhalf[:, 0:2], ALU.pow).then_inc(rs4, 1)

            def squares(n):
                for j in range(HG):
                    pool.wait_ge(gel_ready, HJ * n + j + 1)
                    pool.tensor_tensor(sq[0][:, j, :], gel[j], gel[j], ALU.mult).then_inc(sq_ready[0], 1)

            def add_squares(n):
                pool.wait_ge(ssq_ready, 2 * n + 2)
                if not_first(n):
                    pool.wait_ge(fo_full, 2 * n)
                pool.tensor_tensor(ssq[:, :], halves[0][:, :], halves[1][:, :], ALU.add).then_inc(ssq_sum, 1)

            def with_c2(n):
                if not_first(n):
                    pool.wait_ge(o_ready, TT * n)
                pool.tensor_tensor(x2c[:, :, :], x2[:, :, :],
                                   c2[:, :].rearrange("p (o d) -> p o d", o=1).to_broadcast([P, TT, D]),
                                   ALU.add).then_inc(x2c_ready, 1)

            deviations(0)
            squares(0)
            with_c2(0)
            with pool.Fori(1, NC) as n:
                with_bias(n)
                add_squares(n - 1)
                deviations(n)
                hidden_deviations(n - 1, 0)
                hidden_deviations(n - 1, 1)
                squares(n)
                with_c2(n)
            add_squares(NC - 1)
            hidden_deviations(NC - 1, 0)
            hidden_deviations(NC - 1, 1)

        @block.scalar
        def _(act):
            prime(act, PB, pv_done)
            prime(act, DMA_PRIME, *y_st)
            act.wait_ge(ctx_full, 1)
            act.activation(ctx_p[:, 0, :, :].rearrange("p m t -> p (m t)"), CT, ACT.Copy).then_inc(ctx_p1, 1)

            def turned_chunk(n):
                act.wait_ge(xT_full, n + 1)
                if not_first(n):
                    act.wait_ge(v_full, TT * n)
                for k in range(KD):
                    act.activation(xnT[:, k, :], XT[:, k, :], ACT.Copy).then_inc(xT_evac, 1)

            def first_parts(n):
                for m in range(2 * KD):
                    act.wait_ge(qk_full, 2 * KD * n + m + 1)
                    if not_first(n):
                        act.wait_ge(qk_st[m], 16 * n)
                    act.activation(parts[m][:, 0, :], QK[m], ACT.Identity, bias=bqk[:, m:m + 1]).then_inc(p1_ready, 1)

            def turned_weights(which):
                for k in range(KD):
                    act.wait_ge(wt_full, KD * which + k + 1)
                    src = WT[k % 2].rearrange("p (j c) -> p j c", c=P)
                    dst = fcT[:, k, :, :] if which == 0 else wT[:, :, k * P:(k + 1) * P]
                    act.activation(dst, src, ACT.Copy).then_inc(wt_read, 1)

            turned_chunk(0)
            act.wait_ge(qkvw_ld, 48)
            first_parts(0)
            turned_chunk(1)
            with act.Fori(1, NC - 1) as n:
                first_parts(n)
                turned_chunk(n + 1)
            turned_weights(0)
            first_parts(NC - 1)
            turned_weights(1)
            act.wait_ge(const_ready, 6)
            for par in range(2):
                act.activation(stk_e[par][KR:KM, :, :].rearrange("r h s -> r (h s)"),
                               ones[KR:KM, 0:1].to_broadcast([KM - KR, HG * SP]), ACT.Copy).then_inc(ones_ready, 1)
            for which, dst in enumerate((c1, c2)):
                act.wait_ge(cc_full, which + 1)
                act.activation(dst[:, :], CC[which], ACT.Copy, scale=(-1.0, 1.0)[which]).then_inc(cc_read, 1)

            def slot(i, u):
                g = 2 * i + u

                def save(c):
                    act.wait_ge(pv_done, PB + NS * g + CEND[c] + 1)
                    act.wait_ge(y_st[c], DMA_PRIME + 16 * g)
                    act.activation(ystage[c][:, :], ACC, ACT.Copy).then_inc(y_ready[c], 1)

                for s, (c, j, col, tok, w) in enumerate(STEPS):
                    rows = P if j < KB - 1 else LAST
                    for k in range(2):
                        act.wait_ge(sc_full[k], PRIME + NS * g + s + 1)
                        act.wait_ge(pv_done, NS * g + s + 1)
                        act.activation(probs[(NS * u + s) % PB][0:rows, 2 * k:2 * k + 2, 0:w], SC[k][0:rows, :, 0:w],
                                       ACT.Exp, scale=HD ** -0.5).then_inc(pr_ready[k], 1)
                    if s == CEND[0] + LAG:
                        save(0)
                save(1)

            with act.Fori(0, NG // 2) as i:
                slot(i, 0)
                slot(i, 1)

            def hidden(n, bank):
                act.wait_ge(ln_full, n + 1)
                for k in range(KD):
                    act.activation(hi[:, k, :], bank[:, k, :], ACT.Copy).then_inc(hi_ready, 1)
                for j in range(HJ + 1):
                    if j < HJ:
                        act.wait_ge(fc_full, HJ * n + j + 1)
                        act.activation(gel[j], FC[j % 2], ACT.Gelu).then_inc(gel_ready, 1)
                    if j > HG:
                        act.wait_ge(gel_ready, HJ * n + j)
                        act.activation(sq[1][:, j - 1 - HG, :], gel[j - 1], ACT.Square).then_inc(sq_ready[1], 1)

            hidden(0, LN0)
            with act.Fori(1, NC) as n:
                hidden(n, LN)

        @block.vector
        def _(dve):
            prime(dve, DMA_PRIME, o_st)
            own = [0]

            def chain(ins, signal=dve_w):
                own[0] += 1
                ins.then_inc(signal, 1)
                dve.wait_ge(signal, own[0])

            dve.wait_ge(ctx_ld, 16 * B)
            dve.tensor_copy(vctx[:, :, :, 0:HD], ctx_t[:, :, :].rearrange("p b (h d) -> p b h d", d=HD))\
                .then_inc(vctx_ready, 1)
            dve.wait_ge(ctx_p1, 1)
            flat = [ctx_p[:, a, :, :].rearrange("p m t -> p (m t)") for a in range(3)]
            chain(dve.tensor_tensor(ctx_r[:, :], CT, flat[0], ALU.subtract))
            dve.tensor_copy(flat[1], ctx_r[:, :]).then_inc(ctx_p2, 1)

            def token_statistics(n):
                dve.wait_ge(x_ld, 16 * n + 16)
                for tt in range(TT):
                    dve.bn_stats(stats[:, tt, :], x_a[:, tt, :]).then_inc(dve_a, 1)
                wait_apart(dve, (dve_a, 2 * TT * n + TT))
                for tt in range(TT):
                    dve.bn_aggr(mv[:, tt, :], stats[:, tt, :]).then_inc(dve_a, 1)
                dve.wait_ge(dve_a, 2 * TT * n + 2 * TT)
                dve.tensor_scalar(ve[:, :], mv[:, :, 1], LN_EPS, None, ALU.add).then_inc(ve_ready, 1)

            def normalise_tokens(n):
                dve.wait_ge(rs_ready, n + 1)
                if not_first(n):
                    dve.wait_ge(xT_full, n)
                for tt in range(TT):
                    dve.tensor_scalar(xn[:, tt, :], x_a[:, tt, :], mv[:, tt, 0:1], rs[:, tt:tt + 1],
                                      ALU.subtract, ALU.mult).then_inc(xn_ready, 1)

            def second_parts(n, tiles):
                for m in tiles:
                    dve.wait_ge(p1_ready, 2 * KD * n + m + 1)
                    if not_first(n):
                        dve.wait_ge(p3_ready, 2 * KD * (n - 1) + m + 1)
                    dve.scalar_tensor_tensor(resid[m][:, :], QK[m], bqk[:, m:m + 1], parts[m][:, 0, :],
                                             ALU.add, ALU.subtract).then_inc(r_ready, 1)
                    dve.wait_ge(r_ready, 2 * KD * n + m + 1)
                    dve.tensor_copy(parts[m][:, 1, :], resid[m][:, :]).then_inc(p2_ready, 1)

            def value_tiles(n):
                for tt in range(TT):
                    dve.wait_ge(v_full, TT * n + tt + 1)
                    if not_first(n):
                        dve.wait_ge(v_st[tt], 16 * n)
                    dve.tensor_tensor(vtile[:, tt, :, 0:HD], VV[tt % 2].rearrange("p (h d) -> p h d", d=HD),
                                      bv[:, :].rearrange("p (h d) -> p h d", d=HD), ALU.add).then_inc(v_ready, 1)

            raw = (raw_fc, raw_out)

            def absolute_sums(which):
                dve.wait_ge((fc_ld, wo_ld)[which], 16)
                dve.tensor_reduce(gam[:, which:which + 1], raw[which], AX.XY, ALU.add, apply_absolute_value=True)\
                    .then_inc(abs_ready, 1)

            def thresholds(which):
                dve.wait_ge(gam_full, which + 1)
                chain(dve.tensor_scalar(gam[:, 2 + which:3 + which], GAM, TERN_EPS, 0.5, ALU.add, ALU.mult))
                chain(dve.tensor_scalar(gam[:, 4 + which:5 + which], gam[:, 2 + which:3 + which], -1.0, None, ALU.mult))

            def ternarise(which):
                r2 = raw[which].rearrange("p a b -> p (a b)")
                dst = (tern_fcv, tern_outv)[which]
                chain(dve.tensor_scalar(tern_a, r2, gam[:, 4 + which:5 + which], None, ALU.is_lt))
                dve.scalar_tensor_tensor(dst.rearrange("p a b -> p (a b)"), r2, gam[:, 2 + which:3 + which],
                                         tern_a, ALU.is_gt, ALU.subtract).then_inc(tern_ready, 1)
                dve.wait_ge(tern_ready, which + 1)

            token_statistics(0)
            normalise_tokens(0)
            absolute_sums(0)
            dve.wait_ge(qkvw_ld, 48)
            dve.wait_ge(ones_ready, 4)
            second_parts(0, (0, 1))
            token_statistics(1)
            second_parts(0, (2, 3))
            thresholds(0)
            normalise_tokens(1)
            value_tiles(0)
            ternarise(0)
            with dve.Fori(1, NC - 1) as n:
                token_statistics(n + 1)
                second_parts(n, (0, 1))
                normalise_tokens(n + 1)
                second_parts(n, (2, 3))
                value_tiles(n)
            absolute_sums(1)
            thresholds(1)
            ternarise(1)
            second_parts(NC - 1, range(2 * KD))
            value_tiles(NC - 1)

            def unit(G, nu):
                qi, slot_, key, w = UNITS[nu]
                c, ti = qi // TT, qi % TT
                start = S - (MEM + P * (qi + 1)) + key
                for h in range(HG):
                    local = item(nu, h)
                    wait_apart(dve, (mx_full, items_before(G - 1, local) + 1))
                    dve.tensor_tensor_reduce(junk[local % MXB][:, 0:w], MX[local % MXB][:, 0:w], window[:, start:start + w],
                                             1.0, LOWEST, ALU.add, ALU.max, mpart[c][:, h, ti, slot_:slot_ + 1])\
                        .then_inc(mx_read, 1)

            def split_max(G, c):
                q = CB * G + c
                dve.wait_ge(mx_read, items_before(G - 1, item((UA if c == 0 else NU) - 1, HG - 1)) + 1)
                dve.tensor_reduce(negm[:, :], mpart[c][:, :, :, :], AX.X, ALU.max, negate=True).then_inc(dve_b, 1)
                dve.wait_ge(dve_b, 4 * q + 1)
                dve.tensor_copy(mparts[:, 0, :], negm[:, :]).then_inc(dve_b, 1)
                dve.wait_ge(dve_b, 4 * q + 2)
                dve.tensor_tensor(mres[:, :], negm[:, :], mparts[:, 0, :], ALU.subtract).then_inc(dve_b, 1)
                dve.wait_ge(dve_b, 4 * q + 3)
                dve.tensor_copy(mparts[:, 1, :], mres[:, :]).then_inc(dve_b, 1)
                dve.wait_ge(dve_b, 4 * q + 4)
                dve.tensor_tensor(mparts[:, 2, :], mres[:, :], mparts[:, 1, :], ALU.subtract).then_inc(mp_ready, 1)

            def rows_out(q, which, g):
                dve.wait_ge(mx_full, items_before(g, rows_item(which)) + 1)
                if not_first(q):
                    dve.wait_ge(mr_st, 16 * q)
                dve.tensor_copy(mrows[:, :], MT[rows_item(which) % MXB]).then_inc(mx_read, 1)

            def invert(b):
                dve.wait_ge(den_ld, 16 * b + 16)
                dve.reciprocal(rden[b][:, :], den[b][:, :]).then_inc(rden_ready, 1)

            def max_pass(G, first_rows):
                for nu in range(NU):
                    unit(G, nu)
                    if nu == ROWS_AT[0] and first_rows is not None:
                        rows_out(first_rows, 0, G - 1)
                    if nu == UA - 1:
                        split_max(G, 0)
                    if nu == ROWS_AT[1]:
                        rows_out(CB * G, 1, G - 1)
                        if isinstance(G, int) and G == NG - 1:
                            invert(0)
                split_max(G, 1)

            dve.wait_ge(const_ready, 6)
            max_pass(0, None)
            with dve.Fori(0, NG // 2 - 1) as i:
                for u in range(2):
                    max_pass(2 * i + u + 1, CB * (2 * i + u) + 1)
            max_pass(NG - 1, CB * (NG - 2) + 1)
            rows_out(CB * (NG - 1) + 1, 0, NG - 1)


            def normalise(n):
                dve.wait_ge(c_ld, 16 * 2 * KD * (n + 1))
                if not_first(n):
                    dve.wait_ge(pj_full, 2 * n)
                dve.tensor_tensor(ynT, yraw, rwide, ALU.mult).then_inc(ynT_ready, 1)

            def second_norm(n):
                dve.wait_ge(xb_ready, n + 1)
                if not_first(n):
                    dve.wait_ge(x2c_ready, n)
                for pair in range(2):
                    tiles = slice(2 * pair, 2 * pair + 2)
                    dve.wait_ge(pj_full, 2 * n + pair + 1)
                    dve.tensor_tensor(x2[:, tiles, :], FC[pair].rearrange("p (t d) -> p t d", d=D), xb[:, tiles, :],
                                      ALU.add).then_inc(x2_ready, 1)
                    dve.wait_ge(x2_ready, 2 * n + pair + 1)
                    for tt in range(2 * pair, 2 * pair + 2):
                        dve.bn_stats(stats[:, tt, :], x2[:, tt, :]).then_inc(dve_x, 1)
                wait_apart(dve, (dve_x, 2 * TT * n + TT))
                for tt in range(TT):
                    dve.bn_aggr(mv[:, tt, :], stats[:, tt, :]).then_inc(dve_x, 1)
                dve.wait_ge(dve_x, 2 * TT * n + 2 * TT)
                dve.tensor_scalar(ve[:, :], mv[:, :, 1], LN_EPS, None, ALU.add).then_inc(ve3, 1)
                dve.wait_ge(rs3, n + 1)
                for tt in range(TT):
                    dve.tensor_scalar(xn[:, tt, :], x2[:, tt, :], mv[:, tt, 0:1], rs[:, tt:tt + 1],
                                      ALU.subtract, ALU.mult).then_inc(xn3, 1)

            def low_parts(n, bank):
                for k in range(KD):
                    dve.wait_ge(hi_ready, KD * n + k + 1)
                    dve.tensor_tensor(lo[:, k, :], bank[:, k, :], hi[:, k, :], ALU.subtract).then_inc(lo_ready, 1)

            def sum_squares(n, half):
                if half == 0 and not_first(n):
                    dve.wait_ge(ssq_sum, n)
                dve.wait_ge(sq_ready[half], HG * n + HG)
                dve.tensor_reduce(halves[half][:, :], sq[half][:, :, :].rearrange("p j t -> p t j"), AX.X,
                                  ALU.add).then_inc(ssq_ready, 1)

            def finish(n, pair):
                if pair == 0:
                    dve.wait_ge(x2c_ready, n + 1)
                    dve.wait_ge(o_st, DMA_PRIME + 16 * n)
                dve.wait_ge(fo_full, 2 * n + pair + 1)
                own_base = 6 * n + 3 * pair
                dve.tensor_copy(moments[pair][:, :, :], FO[:, :, D:D + 2]).then_inc(dve_e, 1)
                dve.wait_ge(dve_e, own_base + 1)
                dve.tensor_tensor(msq[pair][:, :], moments[pair][:, :, 0], moments[pair][:, :, 0], ALU.mult)                    .then_inc(dve_e, 1)
                dve.scalar_tensor_tensor(t1[:, 0, :], c1[:, :], moments[pair][:, 0, 0:1], FO[:, 0, 0:D],
                                         ALU.mult, ALU.add).then_inc(dve_e, 1)
                dve.wait_ge(dve_e, own_base + 2)
                dve.scalar_tensor_tensor(ve_h[pair][:, :], moments[pair][:, :, 1], LN_EPS, msq[pair][:, :],
                                         ALU.add, ALU.subtract).then_inc(ve4, 1)
                dve.scalar_tensor_tensor(t1[:, 1, :], c1[:, :], moments[pair][:, 1, 0:1], FO[:, 1, 0:D],
                                         ALU.mult, ALU.add).then_inc(fo_read, 1)
                dve.wait_ge(dve_e, own_base + 3)
                dve.wait_ge(rs4, 2 * n + pair + 1)
                dve.scalar_tensor_tensor(o_t[:, 2 * pair, :], t1[:, 0, :], rs_h[pair][:, 0:1], x2c[:, 2 * pair, :],
                                         ALU.mult, ALU.add).then_inc(o_ready, 1)
                dve.wait_ge(fo_read, PRIME + 2 * n + pair + 1)
                dve.scalar_tensor_tensor(o_t[:, 2 * pair + 1, :], t1[:, 1, :], rs_h[pair][:, 1:2],
                                         x2c[:, 2 * pair + 1, :], ALU.mult, ALU.add).then_inc(o_ready, 1)
                dve.wait_ge(o_ready, TT * n + 2 * pair + 2)

            normalise(0)
            second_norm(0)
            low_parts(0, LN0)
            invert(1)
            with dve.Fori(1, NC) as n:
                normalise(n)
                sum_squares(n - 1, 0)
                sum_squares(n - 1, 1)
                second_norm(n)
                finish(n - 1, 0)
                low_parts(n, LN)
                finish(n - 1, 1)
            sum_squares(NC - 1, 0)
            sum_squares(NC - 1, 1)
            finish(NC - 1, 0)
            finish(NC - 1, 1)

        @block.tensor
        def _(pe):
            prime(pe, PRIME, *pr_ready, *y_ready, fo_read)
            pe.wait_ge(const_ready, 6)
            pe.wait_ge(ctx_ld, 16 * B)
            for b in range(B):
                for k in range(KD):
                    m = b * KD + k
                    ins = pe.transpose(CT[:, m * MEM:(m + 1) * MEM], ctx_t[:, b, k * P:(k + 1) * P],
                                       ident[0:MEM, 0:MEM])
            ins.then_inc(ctx_full, 1)

            def turn_chunk(n):
                for tt in range(TT):
                    pe.wait_ge(xn_ready, TT * n + tt + 1)
                    for k in range(KD):
                        ins = pe.transpose(XT[:, k, tt * P:(tt + 1) * P], xn[:, tt, k * P:(k + 1) * P], ident[:, :])
                ins.then_inc(xT_full, 1)

            def queries_keys(n):
                pe.wait_ge(xT_evac, KD * n + KD)
                for m in range(2 * KD):
                    if isinstance(n, int) and n == NC - 1 and m in (2, 3):
                        pe.wait_ge(wt_read, m - 1)
                    if not_first(n):
                        pe.wait_ge(r_ready, 2 * KD * (n - 1) + m + 1)
                    for k in range(KD):
                        ins = pe.matmul(QK[m], wqkv[:, k, m * P:(m + 1) * P], xnT[:, k, :],
                                        start=(k == 0), stop=(k == KD - 1))
                    ins.then_inc(qk_full, 1)

            def values(n, tiles):
                for tt in tiles:
                    if not_first(n) or tt >= 2:
                        pe.wait_ge(v_ready, TT * n + tt - 1)
                    for k in range(KD):
                        ins = pe.matmul(VV[tt % 2], xnT[:, k, tt * P:(tt + 1) * P], wqkv[:, k, 2 * D:3 * D],
                                        start=(k == 0), stop=(k == KD - 1))
                    ins.then_inc(v_full, 1)

            def mean_weight(which):
                pe.wait_ge(abs_ready, which + 1)
                pe.matmul(GAM, mean_w[:, :], gam[:, which:which + 1], start=True, stop=True).then_inc(gam_full, 1)

            def turn_weights(which):
                for r in range(KD * which, KD * which + KD):
                    k = r % KD
                    pe.wait_ge(tern_ready, which + 1)
                    pe.wait_ge(r_ready, 2 * KD * (NC - 1 + which))
                    for j in range(HJ):
                        src = tern_fcv[:, j, k * P:(k + 1) * P] if r < KD else tern_outv[:, k, j:H:HJ]
                        ins = pe.transpose(WT[r % 2][:, j * P:(j + 1) * P], src, identt[:, :])
                    ins.then_inc(wt_full, 1)

            def fold_norm(r):
                which, j = r // HJ, r % HJ
                if r == 0:
                    pe.wait_ge(w2_ready, 2)
                lhs, rhs = (ones[:, :], w2[:, j, 0:D]) if which == 0 else (lnb_wide[:, j, :], wT[:, j, :])
                ins = pe.matmul(CC[which], lhs, rhs, start=(j == 0), stop=(j == HJ - 1))
                if j == HJ - 1:
                    ins.then_inc(cc_full, 1)

            turn_chunk(0)
            pe.wait_ge(qkvw_ld, 48)
            queries_keys(0)
            mean_weight(0)
            values(0, range(TT))
            turn_chunk(1)
            with pe.Fori(1, NC - 1) as n:
                queries_keys(n)
                values(n, range(TT))
                turn_chunk(n + 1)
            turn_weights(0)
            pe.wait_ge(xT_evac, KD * NC)
            mean_weight(1)
            queries_keys(NC - 1)
            values(NC - 1, range(TT))
            turn_weights(1)

            def bank_wait(g, local):
                free = bank_free(g, local)
                if not_first(free):
                    pe.wait_ge(mx_read, free)

            def max_head(G, par, nu, h):
                qi, slot_, key, w = UNITS[nu]
                local = item(nu, h)
                bank_wait(G - 1, local)
                pe.matmul(MX[local % MXB][:, 0:w], stq_m[par][0:KR, h, qi * P:(qi + 1) * P],
                          stk_m[par][0:KR, h, key:key + w], start=True, stop=True).then_inc(mx_full, 1)

            def turn_rows(q, which, g):
                local = rows_item(which)
                wait_apart(pe, (mx_read, bank_free(g, local)), (mp_ready, q + 1))
                pe.transpose(MT[local % MXB], mparts[:, :, :].rearrange("p a r -> p (a r)"), identh[:, :])\
                    .then_inc(mx_full, 1)

            def project(n):
                if isinstance(n, int):
                    pe.wait_ge(late_ld, 32)
                pe.wait_ge(ynT_ready, n + 1)
                for tt in range(TT):
                    if not_first(n) and tt % 2 == 0:
                        pe.wait_ge(gel_ready, HJ * n - 1 + tt // 2)
                    for k in range(KD):
                        ins = pe.matmul(FC[tt // 2][:, (tt % 2) * D:(tt % 2 + 1) * D], ynT[:, k, tt * P:(tt + 1) * P],
                                        wpr[:, k, :], start=(k == 0), stop=(k == KD - 1), skip_group_check=True)
                    if tt % 2 == 1:
                        ins.then_inc(pj_full, 1)

            def turn_norm(n, bank):
                for tt in range(TT):
                    pe.wait_ge(xn3, TT * n + tt + 1)
                    for k in range(KD):
                        ins = pe.transpose(bank[:, k, tt * P:(tt + 1) * P], xn[:, tt, k * P:(k + 1) * P], ident[:, :])
                ins.then_inc(ln_full, 1)

            def slot(i, u, more):
                g = 2 * i + u
                pe.wait_ge(e_ld[u], 16 * 2 * (i + 1))
                pe.wait_ge(vs_ld[u], 16 * 2 * (i + 1))
                if more:
                    pe.wait_ge(m_ld[1 - u], 16 * 2 * LOADS * (occ(i, u + 1) + 1))

                def pv(s):
                    c, j, col, tok, w = STEPS[s]
                    rows = P if j < KB - 1 else LAST
                    if j == 0:
                        pe.wait_ge(y_ready[1 - c], PRIME + g + c)
                    for h in range(HG):
                        if h % 2 == 0:
                            if DIAG[s] is None:
                                pe.wait_ge(pr_ready[h // 2], PRIME + NS * g + s + 1)
                            else:
                                done = sum(d is not None for d in DIAG[:s + 1])
                                pe.wait_ge(sel_ready[h // 2], NDIAG * g + done)
                        ins = pe.matmul(ACC[32 * h:32 * h + 32, col:col + w], vst[u][0:rows, j, h, :],
                                        probs[(NS * u + s) % PB][0:rows, h, 0:w], start=(j == 0),
                                        stop=(s == CEND[c]), skip_group_check=True)
                    ins.then_inc(pv_done, 1)

                for s, (c, j, col, tok, w) in enumerate(STEPS):
                    rows = P if j < KB - 1 else LAST
                    if j == 0:
                        pe.wait_ge(mr_ld, 16 * (CB * g + c + 1))
                    if more:
                        max_head(g + 1, 1 - u, s, 0)
                    for k in range(2):
                        pe.wait_ge(pr_ready[k], PRIME + NS * g + s)
                        for h in (2 * k, 2 * k + 1):
                            ins = pe.matmul(SC[k][0:rows, h % 2, 0:w], stk_e[u][0:KM, h, j * P:j * P + rows],
                                            stq_e[u][0:KM, h, tok:tok + w], start=True, stop=True)
                            if h == 2 and more:
                                max_head(g + 1, 1 - u, s, 2)
                        ins.then_inc(sc_full[k], 1)
                        if more:
                            max_head(g + 1, 1 - u, s, 2 * k + 1)
                    if s >= LAG:
                        pv(s - LAG)
                    if s == ROWS_AT[0]:
                        turn_rows(CB * g + 1, 0, g)
                    if s == NS - 3 and not more:
                        project(0)
                    if s == ROWS_AT[1] and more:
                        turn_rows(CB * g + 2, 1, g)
                if not more:
                    turn_norm(0, LN0)
                for s in range(NS - LAG, NS):
                    pv(s)

            pe.wait_ge(m_ld[0], 16 * 2 * LOADS)
            pe.wait_ge(v_ready, TT * NC)
            pe.wait_ge(wt_read, 2 * KD)
            for nu in range(NU):
                for h in range(HG):
                    max_head(0, 0, nu, h)
                    step, rest = divmod(HG * nu + h - FOLD_AT, 2)
                    if rest == 0 and 0 <= step < 2 * HJ:
                        fold_norm(step)
                if nu == ROWS_AT[1]:
                    turn_rows(0, 1, -1)
            pe.wait_ge(cc_read, 2)
            pe.wait_ge(ones_ready, 6)
            with pe.Fori(0, NG // 2 - 1) as i:
                slot(i, 0, True)
                slot(i, 1, True)
            slot(NG // 2 - 1, 0, True)
            slot(NG // 2 - 1, 1, False)

            pe.wait_ge(late_ld, 32)

            def hidden(n):
                pe.wait_ge(hi_ready, KD * n + KD)
                pe.wait_ge(lo_ready, KD * n + KD)
                for j in range(HJ):
                    if j >= 2:
                        pe.wait_ge(gel_ready, HJ * n + j - 1)
                    for k in range(KD):
                        for part in (hi, lo):
                            ins = pe.matmul(FC[j % 2], fcT[:, k, j, :], part[:, k, :],
                                            start=(k == 0 and part is hi), stop=(k == KD - 1 and part is lo))
                    ins.then_inc(fc_full, 1)

            def second(n, tt):
                if tt == 0:
                    pe.wait_ge(gel_ready, HJ * n + HJ)
                if tt % 2 == 0:
                    pe.wait_ge(fo_read, PRIME + 2 * n + tt // 2)
                for j in range(HJ):
                    pe.matmul(FO[:, tt % 2, 0:D + 1], gel[j][:, tt * P:(tt + 1) * P], w2[:, j, 0:D + 1],
                              start=(j == 0), stop=(j == HJ - 1), skip_group_check=True)

            def mean_squares(n, pair):
                if pair == 0:
                    pe.wait_ge(ssq_sum, n + 1)
                for t in range(2):
                    tt = 2 * pair + t
                    ins = pe.matmul(FO[:, t, D + 1:D + 2], ssq[:, tt * P:(tt + 1) * P], w2[:, 0, D:D + 1],
                                    start=False, stop=True, skip_group_check=True)
                ins.then_inc(fo_full, 1)

            hidden(0)
            pe.wait_ge(y_ready[1], PRIME + NG)
            with pe.Fori(1, NC) as n:
                project(n)
                second(n - 1, 0)
                second(n - 1, 1)
                mean_squares(n - 1, 0)
                turn_norm(n, LN)
                second(n - 1, 2)
                second(n - 1, 3)
                mean_squares(n - 1, 1)
                hidden(n)
            for pair in range(2):
                second(NC - 1, 2 * pair)
                second(NC - 1, 2 * pair + 1)
                mean_squares(NC - 1, pair)


_INS = ["x", "ctx_1024", "L0_xattn_W_attn", "L0_xattn_b_attn", "L0_xattn_W_proj", "L0_xattn_b_proj",
        "L0_ffn_W_fc", "L0_ffn_ln_w", "L0_ffn_ln_b", "L0_ffn_W_proj"]


def kernel(**inputs):
    import numpy as _np
    import concourse.bacc as _bacc
    from concourse import mybir as _mybir
    from concourse.bass_utils import run_bass_kernel_spmd as _run

    nc = _bacc.Bacc("TRN2", target_bir_lowering=False, num_devices=1)
    arrays, args = {}, []
    for name in _INS:
        a = _np.ascontiguousarray(inputs[name])
        arrays[f"in_{name}"] = a
        args.append(nc.dram_tensor(f"in_{name}", a.shape, _mybir.dt.from_np(a.dtype), kind="ExternalInput").ap())
    args.append(nc.dram_tensor("out_0", (B, T, D), F32, kind="ExternalOutput").ap())
    build(nc, *args)
    r = _run(nc, [arrays], core_ids=[0])
    return r.results[0]["out_0"]
```
